# Optimizing a Trainium2 kernel written in Bass

```python
import numpy as np
import jax
import jax.numpy as jnp

def _softmax(x, axis=-1):
    return jax.nn.softmax(x, axis=axis)
def _gelu(x):
    return jax.nn.gelu(x, approximate=True)
def _silu(x):
    return jax.nn.silu(x)
def _sigmoid(x):
    return jax.nn.sigmoid(x)
def _layernorm(x, axis=-1, eps=1e-5):
    m = jnp.mean(x, axis=axis, keepdims=True)
    v = jnp.var(x, axis=axis, keepdims=True)
    return (x - m) / jnp.sqrt(v + eps)
def _scatter_add(tgt, idx, src, axis=0):
    return tgt.at[idx].add(src)
def _segment_sum(src, seg, n):
    return jax.ops.segment_sum(src, seg, n)

kernel_name = 'mk_metaformer_d1_conv_nchw128_75cfcd'

def setup_inputs(seed: int = 0):
    np.random.seed(seed)
    _w = jnp.asarray
    def _rec_inputs():
        import jax
        import jax.numpy as jnp
        _gk = jax.random.key(seed)
        x = -0.000125 + 0.9999 * jax.random.normal(jax.random.fold_in(_gk, 1), (256, 128, 32, 32), jnp.float32)
        return x
    x = _rec_inputs()
    def _L0_conv_setup():
        import jax, jax.numpy as jnp
        import numpy as np
        BN_EPS = 1e-05
        NEG_SLOPE = 0.2
        SQRT_D = 1.0
        key = jax.random.key(seed)
        kx, kp = jax.random.split(key)
        B, C, H, W = (256, 128, 32, 32)
        x = jax.random.normal(kx, (B, C, H, W), dtype=jnp.float32)
        P = jax.random.normal(kp, (C, H, H), dtype=jnp.float32)
        lam = jnp.array([0.001], dtype=jnp.float32)
        gamma = jnp.ones((C,), dtype=jnp.float32)
        beta = jnp.zeros((C,), dtype=jnp.float32)
        return {'x': x, 'P': P, 'lam': lam, 'gamma': gamma, 'beta': beta}
    _L0_conv_all = _L0_conv_setup()
    _L0_conv_in = {k: v for k, v in _L0_conv_all.items() if k in ('P', 'lam', 'gamma', 'beta', )}
    del _L0_conv_all

    def _L0_ffn_setup():
        import jax, jax.numpy as jnp
        import numpy as np
        B, S, D, E, H, O, K = (512, 2048, 128, 64, 512, 128, 8)
        key = jax.random.key(seed)
        k0, k1, k2, k3 = jax.random.split(key, 4)
        x = jax.random.normal(k0, (B, S, D), dtype=jnp.float32)
        gate_w = jax.random.normal(k1, (E, D), dtype=jnp.float32) * (1.0 / np.sqrt(D))
        gate_b = jnp.zeros((E,), dtype=jnp.float32)
        weight1 = jax.random.uniform(k2, (E, D + 1, H), dtype=jnp.float32, minval=-1.0, maxval=1.0) * (1.0 / np.sqrt(D + 1))
        weight2 = jax.random.uniform(k3, (E, H + 1, O), dtype=jnp.float32, minval=-1.0, maxval=1.0) * (1.0 / np.sqrt(H + 1))
        return {'x': x, 'gate_w': gate_w, 'gate_b': gate_b, 'weight1': weight1, 'weight2': weight2}
    _L0_ffn_all = _L0_ffn_setup()
    _L0_ffn_in = {k: v for k, v in _L0_ffn_all.items() if k in ('gate_w', 'gate_b', 'weight1', 'weight2', )}
    del _L0_ffn_all

    return {
        "x": x,
        "L0_conv_P": _L0_conv_in["P"],
        "L0_conv_lam": _L0_conv_in["lam"],
        "L0_conv_gamma": _L0_conv_in["gamma"],
        "L0_conv_beta": _L0_conv_in["beta"],
        "L0_ffn_gate_w": _L0_ffn_in["gate_w"],
        "L0_ffn_gate_b": _L0_ffn_in["gate_b"],
        "L0_ffn_weight1": _L0_ffn_in["weight1"],
        "L0_ffn_weight2": _L0_ffn_in["weight2"],
    }

def reference(x, L0_conv_P, L0_conv_lam, L0_conv_gamma, L0_conv_beta, L0_ffn_gate_w, L0_ffn_gate_b, L0_ffn_weight1, L0_ffn_weight2):
    import jax
    import jax.numpy as jnp
    def _L0_conv_ref(x, P, lam, gamma, beta):
        import jax, jax.numpy as jnp
        import numpy as np
        BN_EPS = 1e-05
        NEG_SLOPE = 0.2
        SQRT_D = 1.0
        y = jnp.einsum('bchw,ckh->bckw', x, P)
        y = lam[0] * SQRT_D * y
        y = jnp.where(y >= 0, y, NEG_SLOPE * y)
        mean = jnp.mean(y, axis=(0, 2, 3))
        var = jnp.mean(jnp.square(y), axis=(0, 2, 3)) - jnp.square(mean)
        inv = jax.lax.rsqrt(var + BN_EPS)
        yn = (y - mean[None, :, None, None]) * inv[None, :, None, None]
        return gamma[None, :, None, None] * yn + beta[None, :, None, None]

    def _L0_ffn_ref(x, gate_w, gate_b, weight1, weight2):
        import jax, jax.numpy as jnp
        import numpy as np
        B, S, D, E, H, O, K = (512, 2048, 128, 64, 512, 128, 8)
        Bn, Sn, Dn = x.shape
        logits = jnp.einsum('bsd,ed->bse', x, gate_w) + gate_b
        probs = jax.nn.softmax(logits, axis=1)
        vals, idx = jax.lax.top_k(probs.transpose(0, 2, 1), K)
        topv = vals.transpose(0, 2, 1)
        topi = idx.transpose(0, 2, 1)
        flat_idx = topi.reshape(Bn, K * E)
        gathered = jnp.take_along_axis(x, flat_idx[:, :, None], axis=1)
        gathered = gathered.reshape(Bn, K, E, Dn)
        pooled = jnp.einsum('bked,bke->bed', gathered, topv)
        ones = jnp.ones((E, Bn, 1), dtype=x.dtype)
        h = jnp.concatenate([pooled.transpose(1, 0, 2), ones], axis=-1)
        h = jax.nn.gelu(jnp.einsum('ebd,edh->ebh', h, weight1), approximate=False)
        h = jnp.concatenate([h, ones], axis=-1)
        out = jnp.einsum('ebh,eho->ebo', h, weight2)
        out = out.transpose(1, 0, 2)
        weighted = jnp.einsum('beo,bke->bkeo', out, topv).reshape(Bn, K * E, O)
        outputs = jnp.zeros((Bn, Sn, O), dtype=x.dtype)
        outputs = outputs.at[jnp.arange(Bn)[:, None], flat_idx].add(weighted)
        return outputs

    def _gn(v, G=32, eps=1e-5):
        B_, C_, H_, W_ = v.shape
        g = v.reshape(B_, G, C_ // G, H_, W_)
        m = jnp.mean(g, axis=(2, 3, 4), keepdims=True)
        s = jnp.var(g, axis=(2, 3, 4), keepdims=True)
        return ((g - m) / jnp.sqrt(s + eps)).reshape(v.shape)

    def _ln_c(v, eps=1e-6):
        m = jnp.mean(v, axis=1, keepdims=True)
        s = jnp.var(v, axis=1, keepdims=True)
        return (v - m) / jnp.sqrt(s + eps)

    def _ln_t(v, eps=1e-5):
        m = jnp.mean(v, axis=-1, keepdims=True)
        s = jnp.var(v, axis=-1, keepdims=True)
        return (v - m) / jnp.sqrt(s + eps)

    def _to_tokens(v):
        B_, C_, H_, W_ = v.shape
        return v.reshape(B_, C_, H_ * W_).transpose(0, 2, 1)
    def _from_tokens(t, like):
        B_, C_, H_, W_ = like.shape
        return t.transpose(0, 2, 1).reshape(B_, C_, H_, W_)

    x = x + _L0_conv_ref(_ln_c(x), L0_conv_P, L0_conv_lam, L0_conv_gamma, L0_conv_beta)
    t = _to_tokens(x)
    t = t + _L0_ffn_ref(_ln_t(t), L0_ffn_gate_w, L0_ffn_gate_b, L0_ffn_weight1, L0_ffn_weight2)
    x = _from_tokens(t, x)
    return x


_drawn_inputs = setup_inputs


def setup_inputs(seed=0):
    import zlib

    import numpy as np

    out = dict(_drawn_inputs(seed))
    spreads = {'L0_conv_gamma': (1.0, 0.2), 'L0_conv_beta': (0.0, 0.1), 'L0_ffn_gate_b': (0.0, 0.1)}
    factors = {'L0_ffn_gate_w': 8.0, 'L0_ffn_weight1': 8.0, 'L0_ffn_weight2': 8.0}
    for name, (base, spread) in spreads.items():
        noise = np.random.default_rng([zlib.crc32(name.encode()), seed]).standard_normal(out[name].shape)
        drawn = base * np.exp(spread * noise) if base else spread * noise
        out[name] = jnp.asarray(drawn.astype(out[name].dtype))
    for name, factor in factors.items():
        out[name] = (out[name] * factor).astype(out[name].dtype)
    return out
```

```python
from contextlib import ExitStack

import concourse.bass as bass
from concourse import mybir

F32 = mybir.dt.float32
ALU = mybir.AluOpType
ACT = mybir.ActivationFunctionType
AX = mybir.AxisListType

P = 128
HW = 1024
S = 32
NWB = 8
WQ = 4
GB = 16
CH = 8
NCH = P // CH
E = 64
K8 = 8
HID = 512
HC = HID // P
NEG_SLOPE = 0.2
ON_ACT = (8, 8)
EPS_C, EPS_BN, EPS_T = 1e-6, 1e-5, 1e-5
RING = 4
assert NCH == GB


def n_norm_dve(g, i):
    even, odd = (1 if n < NWB else 0 for n in ON_ACT)
    if i < 0:
        i, g = i + GB, g - 1
    return (even + odd) * (GB // 2) * g + even * ((i + 1) // 2) + odd * (i // 2)


def wait_for(eng, semaphore, count):
    if isinstance(count, int) and count <= 0:
        return
    eng.wait_ge(semaphore, count)


def metaformer_kernel(nc, x, conv_p, lam, gamma, beta, gate_w, gate_b, weight1, weight2, out):
    B = x.shape[0]
    G = B // GB
    NP = B // 2
    assert G % 2 == 0 and G >= 6 and NP % RING == 0

    x_c = x.rearrange("b c h w -> b c (h w)")
    out_c = out.rearrange("b c h w -> b c (h w)")

    y_dram = nc.dram_tensor("y_scratch", (B, P, HW), F32, kind="Internal").ap()
    x1_dram = nc.dram_tensor("x1_scratch", (B, P, HW), F32, kind="Internal").ap()
    m_dram = nc.dram_tensor("m_scratch", (NP, P, HW), F32, kind="Internal").ap()

    with ExitStack() as ctx:
        def sb(name, shape):
            return ctx.enter_context(nc.sbuf_tensor(name, shape, F32))

        def sem(name):
            return ctx.enter_context(nc.semaphore(name))

        arena_w = sb("arena_w", [P, P * P])
        pw = arena_w[:, :].rearrange("p (c m) -> p c m", c=P)
        pooled = arena_w[:, 0:B * E].rearrange("p (b e) -> p b e", e=E)
        arena_g = sb("arena_g", [P, 2 * GB * HW])
        grp = [arena_g[:, i * GB * HW:(i + 1) * GB * HW].rearrange("p (b c w) -> p b c w", b=GB, c=P)
               for i in range(2)]
        cursor = [0]

        def carve(n):
            a = cursor[0]
            cursor[0] += n
            assert cursor[0] <= 2 * GB * HW
            return arena_g[:, a:a + n]

        p_rows = arena_g[0:S, GB * HW:GB * HW + P * S]
        p_cols = arena_g[0:S, GB * HW + P * S:GB * HW + 2 * P * S]
        xin = [sb(f"xin{i}", [P, HW]) for i in range(2)]
        spread = sb("spread", [S, P])
        col_mask = sb("col_mask", [P, WQ])
        ident = sb("ident", [P, P])
        ones = sb("ones", [P, 1])
        neg_half = sb("neg_half", [P, 16])
        lam_col = sb("lam_col", [P, 1])
        gamma_col = sb("gamma_col", [P, 1])
        beta_col = sb("beta_col", [P, 1])
        gate_b_col = sb("gate_b_col", [P, 1])
        ln_st = [sb(f"ln_st{i}", [P, NWB, 3]) for i in range(2)]
        ln_var = [sb(f"ln_var{i}", [P, NWB]) for i in range(2)]
        ln_r = [sb(f"ln_r{i}", [P, NWB]) for i in range(2)]
        ln_nmr = [sb(f"ln_nmr{i}", [P, NWB]) for i in range(2)]
        y_st = [sb(f"y_st{i}", [P, P, 3]) for i in range(2)]
        acc_mean = sb("acc_mean", [P, P])
        acc_m2 = sb("acc_m2", [P, P])
        acc_sq = sb("acc_sq", [P, P])
        sq = sb("sq", [P, P])
        bn = sb("bn", [P, 8])
        bn_a, bn_b = bn[:, 6:7], bn[:, 7:8]

        xb = [carve(2 * HW).rearrange("p (b s) -> p b s", b=2) for _ in range(2)]
        yb = [carve(2 * HW).rearrange("p (b c w) -> p b c w", b=2, c=P) for _ in range(2)]
        x1 = [carve(2 * HW).rearrange("p (b s) -> p b s", b=2) for _ in range(2)]
        x1t = [carve(2 * HW).rearrange("p (b k c) -> p b k c", b=2, k=8) for _ in range(2)]
        tb = [carve(HW) for _ in range(2)]
        ls = carve(HW).rearrange("p (k m) -> p k m", k=8)
        ex = carve(HW)
        pr = carve(HW)
        p0 = carve(HW)
        mm_ = [carve(HW) for _ in range(2)]
        mt = carve(HW).rearrange("p (k m) -> p k m", k=8)
        mx8 = carve(K8)
        ex8 = carve(K8)
        pr8 = carve(K8)
        small = carve(8)
        st2 = [carve(48).rearrange("p (b k t) -> p b k t", b=2, k=8) for _ in range(2)]
        var2 = carve(16).rearrange("p (k b) -> p k b", k=8)
        r2 = [carve(16) for _ in range(2)]
        gate_rows = carve(P)
        gate_cen = carve(P)
        gate_mean = carve(8)
        gwt = carve(E)
        b1_rows = carve(HID)
        b2_rows = carve(P)
        b1t = carve(HC * E).rearrange("p (k e) -> p k e", k=HC)
        b2t = carve(E)
        cmat = carve(P)
        w1 = [carve(HID) for _ in range(2)]
        w2 = [carve(HC * P).rearrange("p (k o) -> p k o", k=HC) for _ in range(2)]
        pc = [carve(B) for _ in range(2)]
        hb = [carve(HC * B).rearrange("p (k b) -> p k b", k=HC) for _ in range(2)]
        cursor[0] = 0
        x4 = [carve(2 * HW).rearrange("p (b s) -> p b s", b=2) for _ in range(RING)]
        m4 = [carve(HW) for _ in range(RING)]
        stg = [carve(P) for _ in range(2)]
        oe = [carve(P) for _ in range(2)]

        ps = ctx.enter_context(nc.psum_tensor("ps", [P, 8 * 512], F32))

        def banks(a, n):
            return ps[:, a * 512:(a + n) * 512]

        const_here = sem("const_here")
        p_here = sem("p_here")
        p_turned = sem("p_turned")
        spread_done = sem("spread_done")
        pw_spread = sem("pw_spread")
        pw_done = sem("pw_done")
        ident_done = sem("ident_done")
        ones_done = sem("ones_done")
        x_here = [sem(f"x_here{i}") for i in range(2)]
        x_turned = sem("x_turned")
        ln_stats = sem("ln_stats")
        ln_v = sem("ln_v")
        ln_rdone = sem("ln_rdone")
        ln_ndone = sem("ln_ndone")
        norm_act = sem("norm_act")
        norm_dve = sem("norm_dve")
        z_ready = sem("z_ready")
        v_done = sem("v_done")
        y_done = sem("y_done")
        y_stats = sem("y_stats")
        y_sq = sem("y_sq")
        y_acc = sem("y_acc")
        y_out = [sem(f"y_out{i}") for i in range(4)]

        bn_step = sem("bn_step")
        bn_sum = sem("bn_sum")
        bn_rs = sem("bn_rs")
        gate_here = sem("gate_here")
        gate_step = sem("gate_step")
        cmat_step = sem("cmat_step")
        turned_small = sem("turned_small")
        small_copied = sem("small_copied")

        xb_here = [sem(f"xb_here{i}") for i in range(2)]
        yb_here = [sem(f"yb_here{i}") for i in range(2)]
        x1_out = [sem(f"x1_out{i}") for i in range(2)]
        m_out = [sem(f"m_out{i}") for i in range(2)]
        ty_ready = sem("ty_ready")
        t_ready = sem("t_ready")
        x1_dve = sem("x1_dve")
        x1_pool = sem("x1_pool")
        tx_ready = sem("tx_ready")
        tx_copied = sem("tx_copied")
        tx_stats = sem("tx_stats")
        v_ready = sem("v_ready")
        r_ready = sem("r_ready")
        l_ready = sem("l_ready")
        ls_done = sem("ls_done")
        lt_ready = sem("lt_ready")
        max_done = sem("max_done")
        nb_step = sem("nb_step")
        nb_ready = sem("nb_ready")
        e_done = sem("e_done")
        e8_done = sem("e8_done")
        inv_ready = sem("inv_ready")
        p_ready = sem("p_ready")
        match_done = sem("match_done")
        m_ready = sem("m_ready")
        mt_ready = sem("mt_ready")
        mt_taken = sem("mt_taken")
        pool_ready = sem("pool_ready")
        pool_taken = sem("pool_taken")

        w_here = [sem(f"w_here{i}") for i in range(2)]
        c_ready = sem("c_ready")
        pc_done = sem("pc_done")
        h_ready = sem("h_ready")
        g_ready = sem("g_ready")
        o_ready = sem("o_ready")
        o_taken = sem("o_taken")

        l4_here = [sem(f"l4_here{i}") for i in range(RING)]
        out_here = [sem(f"out_here{i}") for i in range(RING)]
        stg_done = sem("stg_done")
        tr_ready = sem("tr_ready")
        oe_done = sem("oe_done")
        f_ready = sem("f_ready")
        added = sem("added")

        block = ctx.enter_context(nc.Block())

        def run_phase1(eng, stage, between=None):
            stage(None, 0, 0, 0)
            if between:
                between()
            stage(0, 0, 1, 1)
            stage(1, 1, 2, 0)
            with eng.Fori(1, G // 2 - 1) as j:
                stage(2 * j, 0, 2 * j + 1, 1)
                stage(2 * j + 1, 1, 2 * j + 2, 0)
            stage(G - 2, 0, G - 1, 1)
            stage(G - 1, 1, None, 0)

        def run_phase2(eng, step):
            step(-1, -1, 1, early=True, mid=False, late=False)
            step(0, 0, 0, early=True, mid=True, late=False)
            step(1, 0, 1, early=True, mid=True, late=True)
            step(2, 1, 0, early=True, mid=True, late=True)
            with eng.Fori(1, NP // 2 - 1) as j:
                step(2 * j + 1, j, 1, early=True, mid=True, late=True)
                step(2 * j + 2, j + 1, 0, early=True, mid=True, late=True)
            step(NP - 1, NP // 2 - 1, 1, early=False, mid=True, late=True)
            step(NP, NP // 2, 0, early=False, mid=False, late=True)

        def run_phase3(eng, step):
            step(0, 0, 0, True)
            step(1, 0, 1, True)
            with eng.Fori(1, E // 2 - 1) as j:
                step(2 * j, j, 0, True)
                step(2 * j + 1, j, 1, True)
            step(E - 2, E // 2 - 1, 0, True)
            step(E - 1, E // 2 - 1, 1, False)

        def run_phase4(eng, step):
            for i in range(RING):
                step(i, 0, i, i)
            with eng.Fori(1, NP // RING) as j:
                for i in range(RING):
                    step(RING * j + i, j, i, RING + i)

        @block.sync
        def _(sp):
            sp.dma_start(p_rows.rearrange("k (c h) -> k c h", c=P), conv_p.rearrange("c k h -> k c h")).then_inc(p_here, 16)
            sp.dma_start(lam_col[:, :], lam.rearrange("(a n) -> a n", a=1).to_broadcast((P, 1))).then_inc(const_here, 16)
            sp.dma_start(gamma_col[:, :], gamma.rearrange("(p a) -> p a", a=1)).then_inc(const_here, 16)
            sp.dma_start(beta_col[:, :], beta.rearrange("(p a) -> p a", a=1)).then_inc(const_here, 16)
            for i in range(2):
                sp.dma_start(gate_b_col[E * i:E * i + E, :],
                             gate_b.rearrange("(p a) -> p a", a=1)).then_inc(const_here, 16)

            def store_y(g, gp, i):
                if i == 0:
                    wait_for(sp, y_done, NCH * g + NCH)
                    wait_for(sp, y_stats, NCH * g + NCH)
                wait_for(sp, y_out[i % 4], 16 * (g * (GB // 4) + i // 4))
                sp.dma_start(y_dram[g * GB + i, :, :].unsqueeze(0).rearrange("a p s -> p (a s)"),
                             grp[gp][:, i, :, :].rearrange("p c w -> p (c w)")).then_inc(y_out[i % 4], 16)

            def stage(gc, cp, gf, fp):
                for i in range(GB):
                    if gf is not None:
                        wait_for(sp, x_turned, gf * GB + i - 1)
                        sp.dma_start(xin[i % 2][:, :], x_c[gf * GB + i, :, :]).then_inc(x_here[i % 2], 16)
                    if gc is not None and not (isinstance(gc, int) and gc == 0):
                        store_y(gc - 1, 1 - cp, i)

            run_phase1(sp, stage)
            for i in range(GB):
                store_y(G - 1, 1, i)
            for i in range(4):
                wait_for(sp, y_out[i], 16 * (B // 4))

            sp.dma_start(gate_rows[0:E, :], gate_w).then_inc(gate_here, 16)
            sp.dma_start(b1_rows[0:E, :], weight1[:, P, :]).then_inc(gate_here, 16)
            sp.dma_start(b2_rows[0:E, :], weight2[:, HID, :]).then_inc(gate_here, 16)

            def load(q, qp):
                wait_for(sp, x1_dve, q - 1)
                wait_for(sp, x1_pool, q - 1)
                wait_for(sp, ty_ready, 2 * q - 2)
                sp.dma_start(xb[qp], x_c[bass.ds(2 * q, 2), :, :].rearrange("b c s -> c b s")).then_inc(xb_here[qp], 16)
                sp.dma_start(yb[qp].rearrange("p b c w -> p b (c w)"),
                             y_dram[bass.ds(2 * q, 2), :, :].rearrange("b p s -> p b s")).then_inc(yb_here[qp], 16)

            def store_x1(q, qp):
                wait_for(sp, x1_dve, q + 1)
                wait_for(sp, x1_pool, q + 1)
                sp.dma_start(x1_dram[bass.ds(2 * q, 2), :, :].rearrange("b c s -> c b s"), x1[qp]).then_inc(x1_out[qp], 16)

            def store_m(q, qp):
                wait_for(sp, m_ready, q + 1)
                sp.dma_start(m_dram[q, :, :], mm_[qp]).then_inc(m_out[qp], 16)

            for q in range(4):
                load(q, q % 2)
                if q >= 1:
                    store_x1(q - 1, (q - 1) % 2)
                if q >= 3:
                    store_m(q - 3, (q - 3) % 2)
            with sp.Fori(2, NP // 2) as j:
                for i in range(2):
                    load(2 * j + i, i)
                    store_x1(2 * j + i - 1, 1 - i)
                    store_m(2 * j + i - 3, 1 - i)
            store_x1(NP - 1, 1)
            for q in range(NP - 3, NP):
                store_m(q, q % 2)

            def load_w(e, ep):
                wait_for(sp, h_ready, HC * (e - 1))
                wait_for(sp, o_ready, e - 1)
                sp.dma_start(w1[ep], weight1[e, 0:P, :]).then_inc(w_here[ep], 16)
                sp.dma_start(w2[ep], weight2[e, 0:HID, :].rearrange("(k p) o -> p k o", p=P)).then_inc(w_here[ep], 16)

            load_w(0, 0)
            load_w(1, 1)
            with sp.Fori(1, E // 2) as j:
                load_w(2 * j, 0)
                load_w(2 * j + 1, 1)

            for i in range(2):
                wait_for(sp, x1_out[i], 16 * (NP // 2))
                wait_for(sp, m_out[i], 16 * (NP // 2))
            wait_for(sp, o_taken, E)

            def load4(p, j, i, first):
                wait_for(sp, out_here[i], 16 * j)
                sp.dma_start(x4[i], x1_dram[bass.ds(2 * p, 2), :, :].rearrange("b c s -> c b s")).then_inc(l4_here[i], 16)
                sp.dma_start(m4[i], m_dram[p, :, :]).then_inc(l4_here[i], 16)

            run_phase4(sp, load4)
            for i in range(RING):
                wait_for(sp, out_here[i], 16 * (NP // RING))

        @block.tensor
        def _(pe):
            psx = [banks(0, 2).rearrange("p (k c) -> p k c", k=NWB), banks(2, 2).rearrange("p (k c) -> p k c", k=NWB)]
            psz = [banks(4, 2).rearrange("p (c n) -> p c n", c=CH), banks(6, 2).rearrange("p (c n) -> p c n", c=CH)]

            def turn_image(g, i):
                n = g * GB + i
                wait_for(pe, x_here[i % 2], 16 * (g * (GB // 2) + i // 2 + 1))
                wait_for(pe, norm_act, n - 1)
                if ON_ACT[i % 2] < NWB:
                    wait_for(pe, norm_dve, n_norm_dve(g, i - 1))
                for k in range(NWB):
                    last = pe.transpose(psx[i % 2][:, k, :], xin[i % 2][:, k:HW:NWB], ident[:, :])
                last.then_inc(x_turned, 1)

            def conv_chunk(g, gp, i):
                m = g * NCH + i
                if i == 0:
                    wait_for(pe, norm_act, GB * g + GB)
                    wait_for(pe, norm_dve, n_norm_dve(g, GB))
                wait_for(pe, v_done, m - 1)
                for c in range(CH):
                    last = pe.matmul(psz[i % 2][:, c, :], pw[:, i * CH + c, :], grp[gp][:, :, i * CH + c, :],
                                     start=True, stop=True)
                last.then_inc(z_ready, 1)

            def stage(gc, cp, gf, fp):
                for i in range(GB):
                    if gf is not None:
                        turn_image(gf, i)
                    if gc is not None:
                        conv_chunk(gc, cp, i)

            pe.wait_ge(ident_done, 2)

            def spread_weights():
                pe.wait_ge(p_turned, 1)
                pe.wait_ge(spread_done, 2)
                for q in range(P // 16):
                    wait_for(pe, pw_done, q - 3)
                    pe.matmul(banks(4 + q % 4, 1), spread[:, :], p_cols[:, q * 512:q * 512 + 512],
                              start=True, stop=True).then_inc(pw_spread, 1)
                pe.wait_ge(pw_done, P // 16)

            run_phase1(pe, stage, spread_weights)

            pe.wait_ge(bn_step, 1)
            pe.wait_ge(y_acc, 3 * G)
            pe.wait_ge(ones_done, 1)
            pe.matmul(banks(0, 1)[:, 0:1], acc_mean[:, :], ones[:, :], start=True, stop=True)
            pe.matmul(banks(0, 1)[:, 1:2], acc_sq[:, :], ones[:, :], start=True, stop=True).then_inc(bn_sum, 1)
            pe.wait_ge(gate_step, 3)
            pe.wait_ge(gate_here, 48)
            pe.transpose(banks(2, 1)[:, 0:E], gate_cen[0:E, :], ident[0:E, 0:E])
            for k in range(HC):
                pe.transpose(banks(3, 1)[:, k * E:k * E + E], b1_rows[0:E, k * P:k * P + P], ident[0:E, 0:E])
            pe.transpose(banks(2, 1)[:, E:2 * E], b2_rows[0:E, :], ident[0:E, 0:E]).then_inc(turned_small, 1)
            pe.wait_ge(small_copied, 3)
            pe.wait_ge(bn_step, 2)

            psy = banks(0, 2)
            pst = banks(2, 2).rearrange("p (k c) -> p k c", k=8)
            psm = banks(4, 2).rearrange("p (k m) -> p k m", k=8)
            pslt = banks(6, 2)

            def step(p, ph, par, early, mid, late):
                o = 1 - par
                for b in range(2):
                    if mid:
                        if b == 0:
                            wait_for(pe, x1_dve, p + 1)
                        else:
                            wait_for(pe, x1_pool, p + 1)
                        wait_for(pe, tx_copied, 2 * p + b)
                        for k in range(8):
                            last = pe.transpose(pst[:, k, :], x1[par][:, b, k * P:k * P + P], ident[:, :])
                        last.then_inc(tx_ready, 1)
                    if early:
                        if b == 0:
                            wait_for(pe, yb_here[o], 16 * (ph + par + 1))
                        wait_for(pe, t_ready, 2 * p + 2 + b)
                        for k in range(NWB):
                            last = pe.transpose(psy[:, k * P:k * P + P], yb[o][:, b, :, k], ident[:, :])
                        last.then_inc(ty_ready, 1)
                if late:
                    wait_for(pe, m_ready, p)
                    wait_for(pe, ls_done, p)
                    for k in range(8):
                        last = pe.transpose(psm[:, k, :], mm_[o][:, k * P:k * P + P], ident[:, :])
                    last.then_inc(mt_ready, 1)
                    wait_for(pe, mt_taken, p)
                if mid:
                    for b in range(2):
                        for k in range(8):
                            last = pe.matmul(psm[:, k, b * E:b * E + E], x1[par][:, b, k * P:k * P + P], gwt,
                                             start=True, stop=True)
                    last.then_inc(l_ready, 1)
                if late:
                    wait_for(pe, e_done, p)
                    wait_for(pe, max_done, p)
                    wait_for(pe, mt_taken, p)
                    wait_for(pe, tx_copied, 2 * p)
                    for b in range(2):
                        for k in range(8):
                            last = pe.matmul(pslt[:, b * E:b * E + E], x1t[o][:, b, k, :], mt[:, k, b * E:b * E + E],
                                             start=(k == 0), stop=(k == 7))
                    last.then_inc(pool_ready, 1)
                if mid:
                    wait_for(pe, ls_done, p + 1)
                    if late:
                        wait_for(pe, pool_taken, p)
                    for k in range(8):
                        last = pe.transpose(pslt[:, k * P:k * P + P], ls[:, k, :], ident[:, :])
                    last.then_inc(lt_ready, 1)

            run_phase2(pe, step)

            psc = [banks(0, 1)[:, 0:B], banks(1, 1)[:, 0:B]]
            psh = [banks(2, 2).rearrange("p (k b) -> p k b", k=HC), banks(4, 2).rearrange("p (k b) -> p k b", k=HC)]
            pso = [banks(6, 1)[:, 0:B], banks(7, 1)[:, 0:B]]

            def centre(e, ep):
                wait_for(pe, pc_done, e - 1)
                pe.matmul(psc[ep], cmat, pooled[:, :, e], start=True, stop=True).then_inc(c_ready, 1)

            def hidden(e, eh, ep):
                wait_for(pe, w_here[ep], 32 * (eh + 1))
                wait_for(pe, pc_done, e + 1)
                wait_for(pe, g_ready, HC * (e - 1))
                for k in range(HC):
                    pe.matmul(psh[ep][:, k, 0:B], w1[ep][:, k * P:k * P + P], pc[ep],
                              start=True, stop=True).then_inc(h_ready, 1)

            def expert(e, eh, ep, more):
                if more:
                    centre(e + 1, 1 - ep)
                wait_for(pe, o_taken, e - 1)
                for k in range(HC):
                    wait_for(pe, g_ready, HC * e + k + 1)
                    last = pe.matmul(pso[ep], w2[ep][:, k, :], hb[ep][:, k, :], start=(k == 0), stop=(k == HC - 1))
                last.then_inc(o_ready, 1)
                if more:
                    hidden(e + 1, eh + ep, 1 - ep)

            pe.wait_ge(pool_taken, NP)
            pe.wait_ge(cmat_step, 1)
            centre(0, 0)
            hidden(0, 0, 0)
            expert(0, 0, 0, True)
            expert(1, 0, 1, True)
            with pe.Fori(1, E // 2 - 1) as j:
                expert(2 * j, j, 0, True)
                expert(2 * j + 1, j, 1, True)
            expert(E - 2, E // 2 - 1, 0, True)
            expert(E - 1, E // 2 - 1, 1, False)

            trp = [banks(0, 1)[:, 0:P], banks(1, 1)[:, 0:P]]
            psf = banks(4, 4).rearrange("p (b s) -> p b s", b=2)

            def turn_out(p, par):
                wait_for(pe, stg_done, p + 1)
                wait_for(pe, oe_done, p - 1)
                pe.transpose(trp[par], stg[par], ident[:, :]).then_inc(tr_ready, 1)

            def step4(p, j, i, first):
                par = i % 2
                turn_out(p, par)
                wait_for(pe, l4_here[i], 32 * (j + 1))
                wait_for(pe, oe_done, p + 1)
                for b in range(2):
                    wait_for(pe, added, 2 * p + b - 1)
                    for h in range(2):
                        last = pe.matmul(psf[:, b, h * 512:h * 512 + 512], oe[par][b * E:b * E + E, :],
                                         m4[i][b * E:b * E + E, h * 512:h * 512 + 512], start=True, stop=True)
                    last.then_inc(f_ready, 1)

            run_phase4(pe, step4)

        @block.scalar
        def _(act):
            psx = [banks(0, 2).rearrange("p (k c) -> p k c", k=NWB), banks(2, 2).rearrange("p (k c) -> p k c", k=NWB)]
            psz = [banks(4, 2).rearrange("p (c b w) -> p c b w", c=CH, b=GB),
                   banks(6, 2).rearrange("p (c b w) -> p c b w", c=CH, b=GB)]

            def stage(gc, cp, gf, fp):
                for i in range(GB):
                    if gc is not None:
                        wait_for(act, z_ready, gc * NCH + i + 1)
                        for c in range(0, CH, 4):
                            last = act.activation(grp[cp][:, :, i * CH + c:i * CH + c + 4, :].rearrange("p b c w -> p c b w"),
                                                  psz[i % 2][:, c:c + 4, :, :], ACT.Copy, scale=lam_col[:, :])
                        last.then_inc(v_done, 1)
                    if gf is not None:
                        n = gf * GB + i
                        wait_for(act, ln_ndone, n + 1)
                        if not (isinstance(gf, int) and gf < 2):
                            wait_for(act, y_out[i % 4], 16 * ((gf - 2) * (GB // 4) + i // 4 + 1))
                        for k in range(ON_ACT[i % 2]):
                            last = act.activation(grp[fp][:, i, :, k], psx[i % 2][:, k, :], ACT.Identity,
                                                  bias=ln_nmr[i % 2][:, k:k + 1], scale=ln_r[i % 2][:, k:k + 1])
                        last.then_inc(norm_act, 1)

            act.wait_ge(const_here, 16 * 5)
            run_phase1(act, stage, lambda: act.wait_ge(pw_done, P // 16))

            act.wait_ge(turned_small, 1)
            act.activation(gwt, banks(2, 1)[:, 0:E], ACT.Copy).then_inc(small_copied, 1)
            act.activation(b1t.rearrange("p k e -> p (k e)"), banks(3, 1)[:, 0:HC * E], ACT.Copy).then_inc(small_copied, 1)
            act.activation(b2t, banks(2, 1)[:, E:2 * E], ACT.Copy).then_inc(small_copied, 1)

            psy = banks(0, 2)
            pst = banks(2, 2)
            pslt = banks(6, 2)

            def step(p, ph, par, early, mid, late):
                o = 1 - par
                if late:
                    wait_for(act, inv_ready, p)
                    wait_for(act, e8_done, p)
                    wait_for(act, m_ready, p - 1)
                    act.activation(pr, ex, ACT.Copy, scale=small[:, 3:4])
                    act.activation(pr8, ex8, ACT.Copy, scale=small[:, 3:4]).then_inc(p_ready, 1)
                for b in range(2):
                    if early:
                        wait_for(act, ty_ready, 2 * p + 3 + b)
                        if b == 0:
                            wait_for(act, x1_dve, p + 1)
                        else:
                            wait_for(act, x1_pool, p + 1)
                        act.activation(tb[b], psy, ACT.Identity, bias=bn_b, scale=bn_a).then_inc(t_ready, 1)
                    if mid:
                        wait_for(act, tx_ready, 2 * p + b + 1)
                        wait_for(act, pool_ready, p - 1)
                        wait_for(act, tx_stats, 2 * (p - 1))
                        act.activation(x1t[par][:, b, :, :].rearrange("p k c -> p (k c)"), pst, ACT.Copy).then_inc(tx_copied, 1)
                if late:
                    wait_for(act, pool_ready, p)
                    act.activation(pooled[:, bass.ds(2 * (p - 1), 2), :].rearrange("p b e -> p (b e)"),
                                   pslt[:, 0:P], ACT.Copy).then_inc(pool_taken, 1)
                if mid:
                    wait_for(act, nb_ready, p + 1)
                    if late:
                        wait_for(act, p_ready, p)
                        wait_for(act, inv_ready, p)
                    act.activation(ex, pslt, ACT.Exp, bias=small[:, 1:2], accum_out=small[:, 2:3]).then_inc(e_done, 1)
                    act.activation(ex8, mx8, ACT.Exp, bias=small[:, 1:2]).then_inc(e8_done, 1)

            act.wait_ge(bn_step, 6)
            run_phase2(act, step)

            psh = [banks(2, 2).rearrange("p (k b) -> p k b", k=HC), banks(4, 2).rearrange("p (k b) -> p k b", k=HC)]

            def expert(e, eh, ep, more):
                wait_for(act, o_ready, e - 1)
                for k in range(HC):
                    wait_for(act, h_ready, HC * e + 2 * (k // 2) + 2)
                    act.activation(hb[ep][:, k, :], psh[ep][:, k, 0:B], ACT.Gelu,
                                   bias=b1t[:, k, bass.ds(e, 1)]).then_inc(g_ready, 1)

            expert(0, 0, 0, True)
            expert(1, 0, 1, True)
            with act.Fori(1, E // 2) as j:
                expert(2 * j, j, 0, True)
                expert(2 * j + 1, j, 1, True)

            trp = [banks(0, 1)[:, 0:P], banks(1, 1)[:, 0:P]]

            def step4(p, j, i, first):
                par = i % 2
                wait_for(act, tr_ready, p + 1)
                wait_for(act, f_ready, 2 * (p - 1))
                act.activation(oe[par], trp[par], ACT.Copy).then_inc(oe_done, 1)
                if first > 0:
                    store(p - 1, (i - 1) % RING)

            def store(p, i):
                wait_for(act, added, 2 * p + 2)
                act.dma_start(out_c[bass.ds(2 * p, 2), :, :].rearrange("b c s -> c b s"), x4[i]).then_inc(out_here[i], 16)

            run_phase4(act, step4)
            store(NP - 1, RING - 1)

        @block.vector
        def _(dve):
            psx = [banks(0, 2).rearrange("p (k c) -> p k c", k=NWB), banks(2, 2).rearrange("p (k c) -> p k c", k=NWB)]

            dve.memset(ones[:, :], 1.0).then_inc(ones_done, 1)
            dve.memset(neg_half[:, :], -0.5).then_inc(ones_done, 1)
            dve.wait_ge(p_here, 16)
            dve.transpose(p_cols, p_rows).then_inc(p_turned, 1)
            dve.wait_ge(ident_done, 2)
            dve.reduce_sum(col_mask[:, :], ident[:, :].rearrange("p (k q) -> p q k", q=WQ), AX.X).then_inc(p_turned, 1)
            dve.wait_ge(p_turned, 2)

            def spread_weights():
                for q in range(P // 16):
                    dve.wait_ge(pw_spread, q + 1)
                    dve.tensor_tensor(arena_w[:, q * 2048:q * 2048 + 2048].rearrange("p (m q) -> p m q", q=WQ),
                                      banks(4 + q % 4, 1).unsqueeze(2).to_broadcast((P, 512, WQ)),
                                      col_mask[:, :].unsqueeze(1).to_broadcast((P, 512, WQ)), ALU.mult).then_inc(pw_done, 1)
                dve.wait_ge(pw_done, P // 16)

            def stage(gc, cp, gf, fp):
                for i in range(GB):
                    if gc is not None:
                        wait_for(dve, v_done, gc * NCH + i + 1)
                        chunk = grp[cp][:, :, i * CH:i * CH + CH, :].rearrange("p b c w -> p b (c w)")
                        dve.scalar_tensor_tensor(out=chunk, in0=chunk, scalar=NEG_SLOPE, in1=chunk,
                                                 op0=ALU.mult, op1=ALU.max).then_inc(y_done, 1)
                    if gf is not None:
                        n = gf * GB + i
                        q = i % 2
                        wait_for(dve, x_turned, n + 1)
                        for k in range(0, NWB, 2):
                            last = dve.bn_stats(ln_st[q][:, k:k + 2, :].rearrange("p k t -> p (k t)"),
                                                psx[q][:, k:k + 2, :].rearrange("p k c -> p c k"))
                        last.then_inc(ln_stats, 1)
                        wait_for(dve, ln_stats, n + 1)
                        wait_for(dve, ln_rdone, n - 1)
                        dve.tensor_scalar(ln_var[q][:, :], ln_st[q][:, :, 2], 1.0 / P, EPS_C,
                                          ALU.mult, ALU.add).then_inc(ln_v, 1)
                    if gc is not None:
                        if i == 0 and not (isinstance(gc, int) and gc < 2):
                            wait_for(dve, y_acc, 3 * (gc - 1))
                        wait_for(dve, y_done, gc * NCH + i + 1)
                        for c in range(i * CH, i * CH + CH, 2):
                            last = dve.bn_stats(y_st[cp][:, c:c + 2, :].rearrange("p c t -> p (c t)"),
                                                grp[cp][:, :, c:c + 2, :].rearrange("p b c w -> p b w c"))
                        last.then_inc(y_stats, 1)
                    if gf is not None:
                        wait_for(dve, ln_rdone, n + 1)
                        wait_for(dve, norm_act, n - 1)
                        dve.scalar_tensor_tensor(out=ln_nmr[q][:, :], in0=ln_st[q][:, :, 1], scalar=-1.0,
                                                 in1=ln_r[q][:, :], op0=ALU.mult, op1=ALU.mult).then_inc(ln_ndone, 1)
                        if ON_ACT[i % 2] == NWB:
                            continue
                        if not (isinstance(gf, int) and gf < 2):
                            wait_for(dve, y_out[i % 4], 16 * ((gf - 2) * (GB // 4) + i // 4 + 1))
                        for k in range(ON_ACT[i % 2], NWB):
                            last = dve.tensor_scalar(grp[fp][:, i, :, k], psx[q][:, k, :], ln_st[q][:, k, 1:2],
                                                     ln_r[q][:, k:k + 1], ALU.subtract, ALU.mult)
                        last.then_inc(norm_dve, 1)

            run_phase1(dve, stage, spread_weights)

            n_part = GB * NWB
            dve.wait_ge(y_acc, 3 * G)
            dve.scalar_tensor_tensor(out=acc_sq[:, :], in0=acc_m2[:, :], scalar=1.0 / n_part, in1=acc_sq[:, :],
                                     op0=ALU.mult, op1=ALU.add).then_inc(bn_step, 1)
            dve.wait_ge(bn_sum, 1)
            dve.tensor_scalar(bn[:, 0:2], banks(0, 1)[:, 0:2], 1.0 / (P * G), None, ALU.mult).then_inc(bn_step, 1)
            dve.wait_ge(bn_step, 2)
            dve.tensor_tensor(bn[:, 2:3], bn[:, 0:1], bn[:, 0:1], ALU.mult).then_inc(bn_step, 1)
            dve.wait_ge(bn_step, 3)
            dve.tensor_tensor(bn[:, 3:4], bn[:, 1:2], bn[:, 2:3], ALU.subtract).then_inc(bn_step, 1)
            dve.wait_ge(bn_rs, 2)
            dve.tensor_tensor(bn_a, gamma_col[:, :], bn[:, 5:6], ALU.mult).then_inc(bn_step, 1)
            dve.wait_ge(bn_step, 5)
            dve.scalar_tensor_tensor(out=bn[:, 4:5], in0=bn[:, 0:1], scalar=bn_a, in1=beta_col[:, :],
                                     op0=ALU.mult, op1=ALU.subtract).then_inc(bn_rs, 1)
            dve.wait_ge(bn_rs, 3)
            dve.tensor_scalar(bn_b, bn[:, 4:5], -1.0, None, ALU.mult).then_inc(bn_step, 1)

            dve.wait_ge(gate_here, 48)
            dve.reduce_sum(gate_mean[0:E, 0:1], gate_rows[0:E, :], AX.X).then_inc(gate_step, 1)
            dve.wait_ge(gate_step, 1)
            dve.tensor_scalar(gate_mean[0:E, 1:2], gate_mean[0:E, 0:1], 1.0 / P, None, ALU.mult).then_inc(gate_step, 1)
            dve.wait_ge(gate_step, 2)
            dve.tensor_scalar(gate_cen[0:E, :], gate_rows[0:E, :], gate_mean[0:E, 1:2], None,
                              ALU.subtract).then_inc(gate_step, 1)
            dve.tensor_scalar(cmat, ident[:, :], -1.0 / P, None, ALU.add).then_inc(cmat_step, 1)

            psm = banks(4, 2).rearrange("p (m e) -> p m e", e=E)
            pslt = banks(6, 2)

            def wide(r):
                return r.unsqueeze(2).to_broadcast((P, 16, E))

            def step(p, ph, par, early, mid, late):
                o = 1 - par
                if late:
                    wait_for(dve, e_done, p)
                    wait_for(dve, p_ready, p - 1)
                    dve.reciprocal(small[:, 3:4], small[:, 2:3]).then_inc(inv_ready, 1)

                def stats(b):
                    wait_for(dve, tx_copied, 2 * p + b + 1)
                    for k in range(0, 8, 2):
                        last = dve.bn_stats(st2[par][:, b, k:k + 2, :].rearrange("p k t -> p (k t)"),
                                            x1t[par][:, b, k:k + 2, :].rearrange("p k c -> p c k"))
                    last.then_inc(tx_stats, 1)

                if mid:
                    stats(0)
                if late:
                    wait_for(dve, p_ready, p)
                    wait_for(dve, m_ready, p - 1)
                    dve.memset(small[:, 4:5], 0.0)
                    dve.match_replace(out=p0, in_to_replace=pr8, in_values=pr, imm_value=0.0).then_inc(match_done, 1)
                if mid:
                    stats(1)
                    wait_for(dve, tx_stats, 2 * p + 2)
                    wait_for(dve, r_ready, p)
                    dve.tensor_scalar(var2, st2[par][:, :, :, 2].rearrange("p b k -> p k b"), 1.0 / P, EPS_T,
                                      ALU.mult, ALU.add).then_inc(v_ready, 1)
                if early:
                    wait_for(dve, xb_here[o], 16 * (ph + par + 1))
                    wait_for(dve, t_ready, 2 * p + 3)
                    wait_for(dve, x1_out[o], 16 * (ph + par))
                    wait_for(dve, l_ready, p)
                    dve.tensor_tensor(x1[o][:, 0, :].rearrange("p (m k) -> p m k", k=NWB),
                                      tb[0].rearrange("p (k m) -> p m k", k=NWB),
                                      xb[o][:, 0, :].rearrange("p (m k) -> p m k", k=NWB), ALU.add).then_inc(x1_dve, 1)
                if late:
                    wait_for(dve, mt_ready, p)
                    wait_for(dve, pool_ready, p - 1)
                    dve.tensor_tensor(mt.rearrange("p k (b e) -> p (k b) e", e=E), psm, wide(r2[o]), ALU.mult).then_inc(mt_taken, 1)
                if mid:
                    wait_for(dve, l_ready, p + 1)
                    wait_for(dve, r_ready, p + 1)
                    wait_for(dve, lt_ready, p)
                    dve.tensor_tensor(ls.rearrange("p k (b e) -> p (k b) e", e=E), psm, wide(r2[par]), ALU.mult).then_inc(ls_done, 1)
                    wait_for(dve, lt_ready, p + 1)
                    wait_for(dve, e8_done, p)
                    dve.memset(small[:, 4:5], 0.0)
                    dve.max(mx8, pslt).then_inc(max_done, 1)
                    wait_for(dve, max_done, p + 1)
                    dve.tensor_tensor(small[:, 0:1], mx8[:, 0:1], gate_b_col[:, :], ALU.add).then_inc(nb_step, 1)
                    wait_for(dve, nb_step, p + 1)
                    dve.tensor_tensor(small[:, 1:2], gate_b_col[:, :], small[:, 0:1], ALU.subtract).then_inc(nb_ready, 1)

            dve.wait_ge(const_here, 16 * 5)
            dve.wait_ge(bn_step, 6)
            run_phase2(dve, step)

            psc = [banks(0, 1)[:, 0:B], banks(1, 1)[:, 0:B]]
            pso = [banks(6, 1)[:, 0:B], banks(7, 1)[:, 0:B]]

            def take_centred(e, ep):
                wait_for(dve, c_ready, e + 1)
                wait_for(dve, h_ready, HC * (e - 1))
                dve.tensor_copy(pc[ep], psc[ep]).then_inc(pc_done, 1)

            def expert(e, eh, ep, more):
                if more:
                    take_centred(e + 1, 1 - ep)
                wait_for(dve, o_ready, e + 1)
                dve.tensor_scalar(pooled[:, :, e], pso[ep], b2t[:, bass.ds(e, 1)], None, ALU.add).then_inc(o_taken, 1)

            dve.wait_ge(small_copied, 3)
            take_centred(0, 0)
            run_phase3(dve, expert)

            psf = banks(4, 4).rearrange("p (b s) -> p b s", b=2)

            def step4(p, j, i, first):
                wait_for(dve, l4_here[i], 32 * (j + 1))
                for b in range(2):
                    wait_for(dve, f_ready, 2 * p + b + 1)
                    dve.tensor_tensor(x4[i][:, b, :], psf[:, b, :], x4[i][:, b, :], ALU.add).then_inc(added, 1)

            run_phase4(dve, step4)

        @block.gpsimd
        def _(pool):
            pool.memset(ident[:, :], 0.0).then_inc(ident_done, 1)
            pool.wait_ge(ident_done, 1)
            pool.affine_select(out=ident[:, :], in_=ident[:, :], compare_op=ALU.not_equal, fill=1.0,
                               base=0, pattern=[[-1, P]], channel_multiplier=1).then_inc(ident_done, 1)
            pool.memset(spread[:, :], 0.0).then_inc(spread_done, 1)
            pool.wait_ge(spread_done, 1)
            sv = spread[:, :].rearrange("h (k q) -> h k q", q=WQ)
            pool.affine_select(out=sv, in_=sv, compare_op=ALU.not_equal, fill=1.0,
                               base=0, pattern=[[-1, S], [0, WQ]], channel_multiplier=1).then_inc(spread_done, 1)
            for a in (acc_mean, acc_m2, acc_sq):
                pool.memset(a[:, :], 0.0).then_inc(y_sq, 1)

            def stage(gc, cp, gf, fp):
                if gf is not None:
                    for i in range(GB):
                        n = gf * GB + i
                        q = i % 2
                        wait_for(pool, ln_v, n + 1)
                        wait_for(pool, norm_act, n - 1)
                        if ON_ACT[i % 2] < NWB:
                            wait_for(pool, norm_dve, n_norm_dve(gf, i - 1))
                        pool.tensor_tensor(ln_r[q][:, :], ln_var[q][:, :], neg_half[:, 0:NWB], ALU.pow).then_inc(ln_rdone, 1)
                if gc is not None:
                    wait_for(pool, y_stats, NCH * gc + NCH)
                    wait_for(pool, y_acc, 3 * gc)
                    mean = y_st[cp][:, :, 1]
                    pool.tensor_tensor(sq[:, :], mean, mean, ALU.mult).then_inc(y_sq, 1)
                    pool.tensor_tensor(acc_mean[:, :], acc_mean[:, :], mean, ALU.add).then_inc(y_acc, 1)
                    pool.tensor_tensor(acc_m2[:, :], acc_m2[:, :], y_st[cp][:, :, 2], ALU.add).then_inc(y_acc, 1)
                    wait_for(pool, y_sq, gc + 4)
                    pool.tensor_tensor(acc_sq[:, :], acc_sq[:, :], sq[:, :], ALU.add).then_inc(y_acc, 1)

            pool.wait_ge(ones_done, 2)
            pool.wait_ge(y_sq, 3)
            run_phase1(pool, stage)

            pool.wait_ge(bn_step, 4)
            pool.tensor_scalar(bn[:, 4:5], bn[:, 3:4], EPS_BN, None, ALU.add).then_inc(bn_rs, 1)
            pool.wait_ge(bn_rs, 1)
            pool.tensor_tensor(bn[:, 5:6], bn[:, 4:5], neg_half[:, 0:1], ALU.pow).then_inc(bn_rs, 1)

            def step(p, ph, par, early, mid, late):
                o = 1 - par
                if late:
                    wait_for(pool, match_done, p)
                    wait_for(pool, p_ready, p)
                    wait_for(pool, m_out[o], 16 * (ph - (1 - par)))
                    pool.tensor_tensor(mm_[o], pr, p0, ALU.subtract).then_inc(m_ready, 1)
                if mid:
                    wait_for(pool, v_ready, p + 1)
                    wait_for(pool, mt_taken, p - 1)
                    wait_for(pool, ls_done, p - 1)
                    pool.tensor_tensor(r2[par], var2.rearrange("p k b -> p (k b)"), neg_half[:, :], ALU.pow).then_inc(r_ready, 1)
                if early:
                    wait_for(pool, xb_here[o], 16 * (ph + par + 1))
                    wait_for(pool, t_ready, 2 * p + 4)
                    wait_for(pool, x1_out[o], 16 * (ph + par))
                    wait_for(pool, l_ready, p)
                    pool.tensor_tensor(x1[o][:, 1, :].rearrange("p (m k) -> p m k", k=NWB),
                                       tb[1].rearrange("p (k m) -> p m k", k=NWB),
                                       xb[o][:, 1, :].rearrange("p (m k) -> p m k", k=NWB), ALU.add).then_inc(x1_pool, 1)

            run_phase2(pool, step)

            pool.wait_ge(o_taken, E)

            def step4(p, j, i, first):
                par = i % 2
                wait_for(pool, tr_ready, p - 1)
                pool.tensor_copy(stg[par], pooled[:, bass.ds(2 * p, 2), :].rearrange("p b e -> p (b e)")).then_inc(stg_done, 1)

            run_phase4(pool, step4)


_INS = ['x', 'L0_conv_P', 'L0_conv_lam', 'L0_conv_gamma', 'L0_conv_beta', 'L0_ffn_gate_w', 'L0_ffn_gate_b',
        'L0_ffn_weight1', 'L0_ffn_weight2']


def kernel(**inputs):
    import numpy as _np
    import concourse.bacc as _bacc
    from concourse import mybir as _mybir
    from concourse.bass_utils import run_bass_kernel_spmd as _run

    nc = _bacc.Bacc("TRN2", target_bir_lowering=False, num_devices=1)
    arrays, args = {}, []
    for name in _INS:
        a = _np.ascontiguousarray(inputs[name])
        arrays[f"in_{name}_dram"] = a
        args.append(nc.dram_tensor(f"in_{name}_dram", a.shape, _mybir.dt.from_np(a.dtype), kind="ExternalInput").ap())
    shape = inputs['x'].shape
    args.append(nc.dram_tensor("out_0_dram", tuple(shape), _mybir.dt.float32, kind="ExternalOutput").ap())
    metaformer_kernel(nc, *args)
    r = _run(nc, [arrays], core_ids=[0])
    return r.results[0]["out_0_dram"]
```

```python
from contextlib import ExitStack

import concourse.bass as bass
from concourse import mybir

F32 = mybir.dt.float32
ALU = mybir.AluOpType
ACT = mybir.ActivationFunctionType
AX = mybir.AxisListType

P = 128
HW = 1024
S = 32
NWB = 8
WQ = 4
GB = 16
CH = 8
NCH = P // CH
E = 64
K8 = 8
HID = 512
HC = HID // P
NEG_SLOPE = 0.2
EPS_C, EPS_BN, EPS_T = 1e-6, 1e-5, 1e-5
RING = 4
assert NCH == GB


def wait_for(eng, semaphore, count):
    if isinstance(count, int) and count <= 0:
        return
    eng.wait_ge(semaphore, count)


def metaformer_kernel(nc, x, conv_p, lam, gamma, beta, gate_w, gate_b, weight1, weight2, out):
    B = x.shape[0]
    G = B // GB
    NP = B // 2
    assert G % 2 == 0 and G >= 6 and NP % RING == 0

    x_c = x.rearrange("b c h w -> b c (h w)")
    out_c = out.rearrange("b c h w -> b c (h w)")

    y_dram = nc.dram_tensor("y_scratch", (B, P, HW), F32, kind="Internal").ap()
    x1_dram = nc.dram_tensor("x1_scratch", (B, P, HW), F32, kind="Internal").ap()
    m_dram = nc.dram_tensor("m_scratch", (NP, P, HW), F32, kind="Internal").ap()

    with ExitStack() as ctx:
        def sb(name, shape):
            return ctx.enter_context(nc.sbuf_tensor(name, shape, F32))

        def sem(name):
            return ctx.enter_context(nc.semaphore(name))

        arena_w = sb("arena_w", [P, P * P])
        pw = arena_w[:, :].rearrange("p (c m) -> p c m", c=P)
        pooled = arena_w[:, 0:B * E].rearrange("p (b e) -> p b e", e=E)
        arena_g = sb("arena_g", [P, 2 * GB * HW])
        grp = [arena_g[:, i * GB * HW:(i + 1) * GB * HW].rearrange("p (b c w) -> p b c w", b=GB, c=P)
               for i in range(2)]
        cursor = [0]

        def carve(n):
            a = cursor[0]
            cursor[0] += n
            assert cursor[0] <= 2 * GB * HW
            return arena_g[:, a:a + n]

        p_rows = arena_g[0:S, GB * HW:GB * HW + P * S]
        p_cols = arena_g[0:S, GB * HW + P * S:GB * HW + 2 * P * S]
        xin = [sb(f"xin{i}", [P, HW]) for i in range(2)]
        spread = sb("spread", [S, P])
        col_mask = sb("col_mask", [P, WQ])
        ident = sb("ident", [P, P])
        ones = sb("ones", [P, 1])
        neg_half = sb("neg_half", [P, 16])
        lam_col = sb("lam_col", [P, 1])
        gamma_col = sb("gamma_col", [P, 1])
        beta_col = sb("beta_col", [P, 1])
        gate_b_col = sb("gate_b_col", [P, 1])
        ln_st = [sb(f"ln_st{i}", [P, NWB, 3]) for i in range(2)]
        ln_var = [sb(f"ln_var{i}", [P, NWB]) for i in range(2)]
        ln_r = [sb(f"ln_r{i}", [P, NWB]) for i in range(2)]
        ln_neg = [sb(f"ln_neg{i}", [P, NWB]) for i in range(2)]
        ln_nmr = [sb(f"ln_nmr{i}", [P, NWB]) for i in range(2)]
        y_st = [sb(f"y_st{i}", [P, P, 3]) for i in range(2)]
        acc_mean = sb("acc_mean", [P, P])
        acc_m2 = sb("acc_m2", [P, P])
        acc_sq = sb("acc_sq", [P, P])
        sq = sb("sq", [P, P])
        bn = sb("bn", [P, 8])
        inv = sb("inv", [P, NP])
        bn_a, bn_b = bn[:, 6:7], bn[:, 7:8]

        xb = [carve(2 * HW).rearrange("p (b s) -> p b s", b=2) for _ in range(2)]
        yb = [carve(2 * HW).rearrange("p (b c w) -> p b c w", b=2, c=P) for _ in range(2)]
        x1 = [carve(2 * HW).rearrange("p (b s) -> p b s", b=2) for _ in range(2)]
        x1t_even = [carve(HW).rearrange("p (k c) -> p k c", k=8) for _ in range(4)]
        x1t_odd = [carve(HW).rearrange("p (k c) -> p k c", k=8) for _ in range(2)]
        tb = [carve(HW) for _ in range(2)]
        ls = carve(HW).rearrange("p (k m) -> p k m", k=8)
        ex = carve(HW)
        p0 = carve(HW)
        mm_ = [carve(HW) for _ in range(2)]
        mt = carve(HW).rearrange("p (k m) -> p k m", k=8)
        pl = carve(P)
        mx8 = carve(K8)
        ex8 = carve(K8)
        small = carve(8)
        st2 = [carve(24).rearrange("p (k t) -> p k t", k=8) for _ in range(2)]
        var2 = carve(16).rearrange("p (b k) -> p b k", b=2)
        r2 = [carve(16) for _ in range(2)]
        gate_rows = carve(P)
        gate_cen = carve(P)
        gate_mean = carve(8)
        gwt = carve(E)
        b1_rows = carve(HID)
        b2_rows = carve(P)
        b1t = carve(HC * E).rearrange("p (k e) -> p k e", k=HC)
        b2t = carve(E)
        cmat = carve(P)
        w1 = [carve(HID) for _ in range(2)]
        w2 = [carve(HC * P).rearrange("p (k o) -> p k o", k=HC) for _ in range(2)]
        pc = [carve(B) for _ in range(2)]
        hb = [tb[i][:, 0:HC * B].rearrange("p (k b) -> p k b", k=HC) for i in range(2)]
        cursor[0] = 0
        x4 = [carve(2 * HW).rearrange("p (b s) -> p b s", b=2) for _ in range(RING)]
        m4 = [carve(HW) for _ in range(RING)]
        stg = [carve(P) for _ in range(2)]
        oe = [carve(P) for _ in range(2)]

        ps = ctx.enter_context(nc.psum_tensor("ps", [P, 8 * 512], F32))

        def banks(a, n):
            return ps[:, a * 512:(a + n) * 512]

        const_here = sem("const_here")
        p_here = sem("p_here")
        p_turned = sem("p_turned")
        spread_done = sem("spread_done")
        pw_spread = sem("pw_spread")
        pw_done = sem("pw_done")
        ident_done = sem("ident_done")
        ones_done = sem("ones_done")
        x_here = [sem(f"x_here{i}") for i in range(2)]
        x_turned = sem("x_turned")
        ln_stats = sem("ln_stats")
        ln_m = sem("ln_m")
        ln_v = sem("ln_v")
        ln_rdone = sem("ln_rdone")
        ln_ndone = sem("ln_ndone")
        norm_act = sem("norm_act")
        z_ready = sem("z_ready")
        v_done = sem("v_done")
        y_done = sem("y_done")
        y_stats = sem("y_stats")
        y_sq = sem("y_sq")
        y_acc = sem("y_acc")
        y_out = [sem(f"y_out{i}") for i in range(4)]

        bn_step = sem("bn_step")
        bn_sum = sem("bn_sum")
        bn_rs = sem("bn_rs")
        gate_here = sem("gate_here")
        gate_step = sem("gate_step")
        cmat_step = sem("cmat_step")
        turned_small = sem("turned_small")
        small_copied = sem("small_copied")

        xb_here = [sem(f"xb_here{i}") for i in range(2)]
        yb_here = [sem(f"yb_here{i}") for i in range(2)]
        x1_out = [sem(f"x1_out{i}") for i in range(2)]
        m_out = [sem(f"m_out{i}") for i in range(2)]
        ty_ready = sem("ty_ready")
        t_ready = sem("t_ready")
        x1_sum = sem("x1_sum")
        tx_ready = sem("tx_ready")
        tx_copied = sem("tx_copied")
        tx_stats = sem("tx_stats")
        v_ready = sem("v_ready")
        r_ready = sem("r_ready")
        l_ready = sem("l_ready")
        ls_done = sem("ls_done")
        lt_ready = sem("lt_ready")
        max_done = sem("max_done")
        nb_step = sem("nb_step")
        nb_ready = sem("nb_ready")
        e_done = sem("e_done")
        e8_done = sem("e8_done")
        inv_ready = sem("inv_ready")
        match_done = sem("match_done")
        m_ready = sem("m_ready")
        mt_ready = sem("mt_ready")
        mt_taken = sem("mt_taken")
        pool_ready = sem("pool_ready")
        pl_done = sem("pl_done")
        pt_ready = sem("pt_ready")
        pt_taken = sem("pt_taken")

        w_here = [sem(f"w_here{i}") for i in range(2)]
        c_ready = sem("c_ready")
        pc_done = sem("pc_done")
        h_ready = sem("h_ready")
        g_ready = sem("g_ready")
        o_ready = sem("o_ready")
        o_taken = sem("o_taken")

        l4_here = [sem(f"l4_here{i}") for i in range(RING)]
        out_here = [sem(f"out_here{i}") for i in range(RING)]
        stg_done = sem("stg_done")
        tr_ready = sem("tr_ready")
        oe_done = sem("oe_done")
        f_ready = sem("f_ready")
        added = sem("added")

        block = ctx.enter_context(nc.Block())

        def run_phase1(eng, stage, between=None):
            stage(None, 0, 0, 0)
            if between:
                between()
            stage(0, 0, 1, 1)
            stage(1, 1, 2, 0)
            with eng.Fori(1, G // 2 - 1) as j:
                stage(2 * j, 0, 2 * j + 1, 1)
                stage(2 * j + 1, 1, 2 * j + 2, 0)
            stage(G - 2, 0, G - 1, 1)
            stage(G - 1, 1, None, 0)

        def image_ahead(g, i, d):
            if g is None:
                return None
            if i + d < GB:
                return g, i + d
            return None if isinstance(g, int) and g == G - 1 else (g + 1, i + d - GB)

        def run_phase2(eng, step):
            step(-1, -1, 3, early=True, mid=False, late=False, last_=False)
            step(0, 0, 0, early=True, mid=True, late=False, last_=False)
            step(1, 0, 1, early=True, mid=True, late=True, last_=False)
            step(2, 1, 2, early=True, mid=True, late=True, last_=True)
            with eng.Fori(1, NP // 4) as j:
                step(4 * j - 1, 2 * j - 1, 3, early=True, mid=True, late=True, last_=True)
                step(4 * j, 2 * j, 0, early=True, mid=True, late=True, last_=True)
                step(4 * j + 1, 2 * j, 1, early=True, mid=True, late=True, last_=True)
                step(4 * j + 2, 2 * j + 1, 2, early=True, mid=True, late=True, last_=True)
            step(NP - 1, NP // 2 - 1, 3, early=False, mid=True, late=True, last_=True)
            step(NP, NP // 2, 0, early=False, mid=False, late=True, last_=True)
            step(NP + 1, NP // 2, 1, early=False, mid=False, late=False, last_=True)

        def run_phase3(eng, step):
            step(0, 0, 0, True)
            step(1, 0, 1, True)
            with eng.Fori(1, E // 2 - 1) as j:
                step(2 * j, j, 0, True)
                step(2 * j + 1, j, 1, True)
            step(E - 2, E // 2 - 1, 0, True)
            step(E - 1, E // 2 - 1, 1, False)

        def run_phase4(eng, step):
            for i in range(RING):
                step(i, 0, i, i)
            with eng.Fori(1, NP // RING) as j:
                for i in range(RING):
                    step(RING * j + i, j, i, RING + i)

        @block.sync
        def _(sp):
            sp.dma_start(p_rows.rearrange("k (c h) -> k c h", c=P), conv_p.rearrange("c k h -> k c h")).then_inc(p_here, 16)
            sp.dma_start(lam_col[:, :], lam.rearrange("(a n) -> a n", a=1).to_broadcast((P, 1))).then_inc(const_here, 16)
            sp.dma_start(gamma_col[:, :], gamma.rearrange("(p a) -> p a", a=1)).then_inc(const_here, 16)
            sp.dma_start(beta_col[:, :], beta.rearrange("(p a) -> p a", a=1)).then_inc(const_here, 16)
            for i in range(2):
                sp.dma_start(gate_b_col[E * i:E * i + E, :],
                             gate_b.rearrange("(p a) -> p a", a=1)).then_inc(const_here, 16)

            def store_y(g, gp, i):
                if i == 0:
                    wait_for(sp, y_done, NCH * g + NCH)
                    wait_for(sp, y_stats, NCH * g + NCH)
                wait_for(sp, y_out[i % 4], 16 * (g * (GB // 4) + i // 4))
                sp.dma_start(y_dram[g * GB + i, :, :].unsqueeze(0).rearrange("a p s -> p (a s)"),
                             grp[gp][:, i, :, :].rearrange("p c w -> p (c w)")).then_inc(y_out[i % 4], 16)

            def load_x(g, i):
                wait_for(sp, x_turned, g * GB + i - 1)
                sp.dma_start(xin[i % 2][:, :], x_c[g * GB + i, :, :]).then_inc(x_here[i % 2], 16)

            def stage(gc, cp, gf, fp):
                if isinstance(gf, int) and gf == 0:
                    load_x(0, 0)
                    load_x(0, 1)
                for i in range(GB):
                    if image_ahead(gf, i, 2):
                        load_x(*image_ahead(gf, i, 2))
                    if gc is not None and not (isinstance(gc, int) and gc == 0):
                        store_y(gc - 1, 1 - cp, i)

            run_phase1(sp, stage)
            for i in range(GB):
                store_y(G - 1, 1, i)
            for i in range(4):
                wait_for(sp, y_out[i], 16 * (B // 4))

            sp.dma_start(gate_rows[0:E, :], gate_w).then_inc(gate_here, 16)
            sp.dma_start(b1_rows[0:E, :], weight1[:, P, :]).then_inc(gate_here, 16)
            sp.dma_start(b2_rows[0:E, :], weight2[:, HID, :]).then_inc(gate_here, 16)

            def load(q, qp):
                wait_for(sp, x1_sum, 2 * q - 2)
                wait_for(sp, ty_ready, 2 * q - 2)
                sp.dma_start(xb[qp], x_c[bass.ds(2 * q, 2), :, :].rearrange("b c s -> c b s")).then_inc(xb_here[qp], 16)
                sp.dma_start(yb[qp].rearrange("p b c w -> p b (c w)"),
                             y_dram[bass.ds(2 * q, 2), :, :].rearrange("b p s -> p b s")).then_inc(yb_here[qp], 16)

            def store_x1(q, qp):
                wait_for(sp, x1_sum, 2 * q + 2)
                sp.dma_start(x1_dram[bass.ds(2 * q, 2), :, :].rearrange("b c s -> c b s"), x1[qp]).then_inc(x1_out[qp], 16)

            def store_m(q, qp):
                wait_for(sp, m_ready, q + 1)
                sp.dma_start(m_dram[q, :, :], mm_[qp]).then_inc(m_out[qp], 16)

            for q in range(4):
                load(q, q % 2)
                if q >= 1:
                    store_x1(q - 1, (q - 1) % 2)
                if q >= 3:
                    store_m(q - 3, (q - 3) % 2)
            with sp.Fori(2, NP // 2) as j:
                for i in range(2):
                    load(2 * j + i, i)
                    store_x1(2 * j + i - 1, 1 - i)
                    store_m(2 * j + i - 3, 1 - i)
            store_x1(NP - 1, 1)
            for q in range(NP - 3, NP):
                store_m(q, q % 2)

            def load_w(e, ep):
                wait_for(sp, h_ready, HC * (e - 1))
                wait_for(sp, o_ready, e - 1)
                sp.dma_start(w1[ep], weight1[e, 0:P, :]).then_inc(w_here[ep], 16)
                sp.dma_start(w2[ep], weight2[e, 0:HID, :].rearrange("(k p) o -> p k o", p=P)).then_inc(w_here[ep], 16)

            load_w(0, 0)
            load_w(1, 1)
            with sp.Fori(1, E // 2) as j:
                load_w(2 * j, 0)
                load_w(2 * j + 1, 1)

            for i in range(2):
                wait_for(sp, x1_out[i], 16 * (NP // 2))
                wait_for(sp, m_out[i], 16 * (NP // 2))
            wait_for(sp, o_taken, E)

            def load4(p, j, i, first):
                wait_for(sp, out_here[i], 16 * j)
                sp.dma_start(x4[i], x1_dram[bass.ds(2 * p, 2), :, :].rearrange("b c s -> c b s")).then_inc(l4_here[i], 16)
                sp.dma_start(m4[i], m_dram[p, :, :]).then_inc(l4_here[i], 16)

            run_phase4(sp, load4)
            for i in range(RING):
                wait_for(sp, out_here[i], 16 * (NP // RING))

        @block.tensor
        def _(pe):
            psx = [banks(0, 2).rearrange("p (k c) -> p k c", k=NWB), banks(2, 2).rearrange("p (k c) -> p k c", k=NWB)]
            psz = [banks(4, 2).rearrange("p (c n) -> p c n", c=CH), banks(6, 2).rearrange("p (c n) -> p c n", c=CH)]

            def turn_image(g, i):
                n = g * GB + i
                wait_for(pe, x_here[i % 2], 16 * (g * (GB // 2) + i // 2 + 1))
                wait_for(pe, norm_act, n - 1)
                for k in range(NWB):
                    last = pe.transpose(psx[i % 2][:, k, :], xin[i % 2][:, k:HW:NWB], ident[:, :])
                last.then_inc(x_turned, 1)

            def conv_chunk(g, gp, i):
                m = g * NCH + i
                if i == 0:
                    wait_for(pe, norm_act, GB * g + GB)
                wait_for(pe, v_done, m - 1)
                for c in range(CH):
                    last = pe.matmul(psz[i % 2][:, c, :], pw[:, i * CH + c, :], grp[gp][:, :, i * CH + c, :],
                                     start=True, stop=True)
                last.then_inc(z_ready, 1)

            def stage(gc, cp, gf, fp):
                if isinstance(gf, int) and gf == 0:
                    turn_image(0, 0)
                for i in range(GB):
                    if image_ahead(gf, i, 1):
                        turn_image(*image_ahead(gf, i, 1))
                    if gc is not None:
                        conv_chunk(gc, cp, i)

            pe.wait_ge(ident_done, 2)

            def spread_weights():
                pe.wait_ge(p_turned, 1)
                pe.wait_ge(spread_done, 2)
                for q in range(P // 16):
                    wait_for(pe, pw_done, q - 3)
                    pe.matmul(banks(4 + q % 4, 1), spread[:, :], p_cols[:, q * 512:q * 512 + 512],
                              start=True, stop=True).then_inc(pw_spread, 1)
                pe.wait_ge(pw_done, P // 16)

            run_phase1(pe, stage, spread_weights)

            pe.wait_ge(bn_step, 1)
            pe.wait_ge(y_acc, 3 * G)
            pe.wait_ge(ones_done, 1)
            pe.matmul(banks(0, 1)[:, 0:1], acc_mean[:, :], ones[:, :], start=True, stop=True)
            pe.matmul(banks(0, 1)[:, 1:2], acc_sq[:, :], ones[:, :], start=True, stop=True).then_inc(bn_sum, 1)
            pe.wait_ge(gate_step, 3)
            pe.wait_ge(gate_here, 48)
            pe.transpose(banks(2, 1)[:, 0:E], gate_cen[0:E, :], ident[0:E, 0:E])
            for k in range(HC):
                pe.transpose(banks(3, 1)[:, k * E:k * E + E], b1_rows[0:E, k * P:k * P + P], ident[0:E, 0:E])
            pe.transpose(banks(2, 1)[:, E:2 * E], b2_rows[0:E, :], ident[0:E, 0:E]).then_inc(turned_small, 1)
            pe.wait_ge(small_copied, 3)
            pe.wait_ge(bn_step, 2)

            psy = banks(0, 2)
            pst = banks(2, 2).rearrange("p (k c) -> p k c", k=8)
            psm = banks(4, 2).rearrange("p (k m) -> p k m", k=8)
            pslt = banks(6, 2)

            def step(p, ph, quad, early, mid, late, last_):
                par, o = quad % 2, 1 - quad % 2

                def turn_x1(q, x1_q, b):
                    wait_for(pe, x1_sum, 2 * q + b + 1)
                    wait_for(pe, tx_copied, 2 * q + b)
                    for k in range(8):
                        last = pe.transpose(pst[:, k, :], x1_q[:, b, k * P:k * P + P], ident[:, :])
                    last.then_inc(tx_ready, 1)

                def turn_y(b):
                    if b == 0:
                        wait_for(pe, yb_here[o], 16 * (ph + par + 1))
                        wait_for(pe, pl_done, p - 1)
                    wait_for(pe, t_ready, 2 * p + 2 + b)
                    for k in range(NWB):
                        last = pe.transpose(psy[:, k * P:k * P + P], yb[o][:, b, :, k], ident[:, :])
                    last.then_inc(ty_ready, 1)

                def logits(b):
                    wait_for(pe, ls_done, p)
                    for k in range(8):
                        for h in range(0, P, E):
                            last = pe.matmul(psm[h:h + E, k, b * E:b * E + E],
                                             x1[par][:, b, k * P + h:k * P + h + E], gwt, start=True, stop=True)
                    if b == 1:
                        last.then_inc(l_ready, 1)

                if mid:
                    turn_x1(p, x1[par], 1)
                    logits(0)
                if early:
                    turn_y(0)
                if mid:
                    logits(1)
                if last_:
                    wait_for(pe, pl_done, p - 1)
                    wait_for(pe, mt_taken, p - 1)
                    wait_for(pe, tx_copied, 2 * p + 2 if mid else 2 * NP)
                    pe.transpose(pst[:, 0, :], pl, ident[:, :]).then_inc(pt_ready, 1)
                if early:
                    turn_y(1)
                if late:
                    wait_for(pe, m_ready, p)
                    wait_for(pe, tx_copied, 2 * p + 2 if mid else 2 * NP)
                    wait_for(pe, pt_taken, p - 1)
                    for k in range(8):
                        last = pe.transpose(pst[:, k, :], mm_[o][:, k * P:k * P + P], ident[:, :])
                    last.then_inc(mt_ready, 1)
                if mid:
                    wait_for(pe, ls_done, p + 1)
                    wait_for(pe, e_done, p)
                    for k in range(8):
                        last = pe.transpose(pslt[:, k * P:k * P + P], ls[:, k, :], ident[:, :])
                    last.then_inc(lt_ready, 1)
                if early:
                    wait_for(pe, mt_taken, p)
                    turn_x1(p + 1, x1[o], 0)
                if late:
                    wait_for(pe, mt_taken, p)
                    wait_for(pe, t_ready, 2 * p + 4 if early else 2 * NP)
                    wait_for(pe, pl_done, p - 1)
                    for k in range(8):
                        for b, x1t in ((0, x1t_even[(quad - 1) % 4]), (1, x1t_odd[o])):
                            last = pe.matmul(psy[b * E:b * E + E, 0:P], mt[:, k, b * E:b * E + E], x1t[:, k, :],
                                             start=(k == 0), stop=(k == 7))
                    last.then_inc(pool_ready, 1)

            run_phase2(pe, step)

            psc = [banks(0, 1)[:, 0:B], banks(1, 1)[:, 0:B]]
            psh = [banks(2, 2).rearrange("p (k b) -> p k b", k=HC), banks(4, 2).rearrange("p (k b) -> p k b", k=HC)]
            pso = [banks(6, 1)[:, 0:B], banks(7, 1)[:, 0:B]]

            def centre(e, ep):
                wait_for(pe, pc_done, e - 1)
                pe.matmul(psc[ep], cmat, pooled[:, :, e], start=True, stop=True).then_inc(c_ready, 1)

            def hidden(e, eh, ep):
                wait_for(pe, w_here[ep], 32 * (eh + 1))
                wait_for(pe, pc_done, e + 1)
                wait_for(pe, g_ready, HC * (e - 1))
                for k in range(HC):
                    pe.matmul(psh[ep][:, k, 0:B], w1[ep][:, k * P:k * P + P], pc[ep],
                              start=True, stop=True).then_inc(h_ready, 1)

            def expert(e, eh, ep, more):
                if more:
                    centre(e + 1, 1 - ep)
                wait_for(pe, o_taken, e - 1)
                for k in range(HC):
                    wait_for(pe, g_ready, HC * e + k + 1)
                    last = pe.matmul(pso[ep], w2[ep][:, k, :], hb[ep][:, k, :], start=(k == 0), stop=(k == HC - 1))
                last.then_inc(o_ready, 1)
                if more:
                    hidden(e + 1, eh + ep, 1 - ep)

            pe.wait_ge(pt_taken, NP)
            pe.wait_ge(cmat_step, 1)
            centre(0, 0)
            hidden(0, 0, 0)
            expert(0, 0, 0, True)
            expert(1, 0, 1, True)
            with pe.Fori(1, E // 2 - 1) as j:
                expert(2 * j, j, 0, True)
                expert(2 * j + 1, j, 1, True)
            expert(E - 2, E // 2 - 1, 0, True)
            expert(E - 1, E // 2 - 1, 1, False)

            trp = [banks(0, 1)[:, 0:P], banks(1, 1)[:, 0:P]]
            psf = banks(4, 4).rearrange("p (b s) -> p b s", b=2)

            def turn_out(p, par):
                wait_for(pe, stg_done, p + 1)
                wait_for(pe, oe_done, p - 1)
                pe.transpose(trp[par], stg[par], ident[:, :]).then_inc(tr_ready, 1)

            def step4(p, j, i, first):
                par = i % 2
                turn_out(p, par)
                wait_for(pe, l4_here[i], 32 * (j + 1))
                wait_for(pe, oe_done, p + 1)
                for b in range(2):
                    wait_for(pe, added, 2 * p + b - 1)
                    for h in range(2):
                        last = pe.matmul(psf[:, b, h * 512:h * 512 + 512], oe[par][b * E:b * E + E, :],
                                         m4[i][b * E:b * E + E, h * 512:h * 512 + 512], start=True, stop=True)
                    last.then_inc(f_ready, 1)

            run_phase4(pe, step4)

        @block.scalar
        def _(act):
            psx = [banks(0, 2).rearrange("p (k c) -> p k c", k=NWB), banks(2, 2).rearrange("p (k c) -> p k c", k=NWB)]
            psz = [banks(4, 2).rearrange("p (c b w) -> p c b w", c=CH, b=GB),
                   banks(6, 2).rearrange("p (c b w) -> p c b w", c=CH, b=GB)]

            def stage(gc, cp, gf, fp):
                for i in range(GB):
                    if gf is not None:
                        n = gf * GB + i
                        wait_for(act, ln_ndone, n + 1)
                        if not (isinstance(gf, int) and gf < 2):
                            wait_for(act, y_out[i % 4], 16 * ((gf - 2) * (GB // 4) + i // 4 + 1))
                        for k in range(NWB):
                            last = act.activation(grp[fp][:, i, :, k], psx[i % 2][:, k, :], ACT.Identity,
                                                  bias=ln_nmr[i % 2][:, k:k + 1], scale=ln_r[i % 2][:, k:k + 1])
                        last.then_inc(norm_act, 1)
                    if gc is not None:
                        wait_for(act, z_ready, gc * NCH + i + 1)
                        act.activation(grp[cp][:, :, i * CH:i * CH + CH, :].rearrange("p b c w -> p c b w"),
                                       psz[i % 2], ACT.Copy, scale=lam_col[:, :]).then_inc(v_done, 1)

            act.wait_ge(const_here, 16 * 5)
            run_phase1(act, stage, lambda: act.wait_ge(pw_done, P // 16))

            act.wait_ge(turned_small, 1)
            act.activation(gwt, banks(2, 1)[:, 0:E], ACT.Copy).then_inc(small_copied, 1)
            act.activation(b1t.rearrange("p k e -> p (k e)"), banks(3, 1)[:, 0:HC * E], ACT.Copy).then_inc(small_copied, 1)
            act.activation(b2t, banks(2, 1)[:, E:2 * E], ACT.Copy).then_inc(small_copied, 1)

            psy = banks(0, 2)
            pst = banks(2, 2)
            pslt = banks(6, 2)

            def step(p, ph, quad, early, mid, late, last_):
                par, o = quad % 2, 1 - quad % 2

                def scaled_y(b):
                    wait_for(act, ty_ready, 2 * p + 3 + b)
                    wait_for(act, x1_sum, 2 * p + b + 1)
                    act.activation(tb[b], psy, ACT.Identity, bias=bn_b, scale=bn_a).then_inc(t_ready, 1)

                def copy_x1(q, b):
                    wait_for(act, tx_ready, 2 * q + b + 1)
                    wait_for(act, pool_ready, q - 3 if b == 0 else q - 1)
                    wait_for(act, tx_stats, 2 * (q - 3) if b == 0 else 2 * (q - 1))
                    place = x1t_even[(quad + 1) % 4] if b == 0 else x1t_odd[par]
                    act.activation(place.rearrange("p k c -> p (k c)"), pst, ACT.Copy).then_inc(tx_copied, 1)

                if mid:
                    copy_x1(p, 1)
                if early:
                    scaled_y(0)
                if last_:
                    wait_for(act, pt_ready, p - 1)
                    act.activation(pooled[:, bass.ds(2 * (p - 2), 2), :].rearrange("p b e -> p (b e)"),
                                   banks(2, 1)[:, 0:P], ACT.Copy).then_inc(pt_taken, 1)
                if early:
                    scaled_y(1)
                    copy_x1(p + 1, 0)
                if mid:
                    wait_for(act, nb_ready, p + 1)
                    wait_for(act, m_ready, p)
                    wait_for(act, inv_ready, p)
                    act.activation(ex, pslt, ACT.Exp, bias=small[:, 1:2], accum_out=small[:, 2:3]).then_inc(e_done, 1)
                    act.activation(ex8, mx8, ACT.Exp, bias=small[:, 1:2]).then_inc(e8_done, 1)
                if late:
                    wait_for(act, pool_ready, p)
                    wait_for(act, inv_ready, p)
                    wait_for(act, pt_ready, p - 1)
                    act.activation(pl, psy[:, 0:P], ACT.Copy, scale=inv[:, bass.ds(p - 1, 1)]).then_inc(pl_done, 1)

            act.wait_ge(bn_step, 6)
            run_phase2(act, step)

            psh = [banks(2, 2).rearrange("p (k b) -> p k b", k=HC), banks(4, 2).rearrange("p (k b) -> p k b", k=HC)]

            def expert(e, eh, ep, more):
                wait_for(act, o_ready, e - 1)
                for k in range(HC):
                    wait_for(act, h_ready, HC * e + 2 * (k // 2) + 2)
                    act.activation(hb[ep][:, k, :], psh[ep][:, k, 0:B], ACT.Gelu,
                                   bias=b1t[:, k, bass.ds(e, 1)]).then_inc(g_ready, 1)

            expert(0, 0, 0, True)
            expert(1, 0, 1, True)
            with act.Fori(1, E // 2) as j:
                expert(2 * j, j, 0, True)
                expert(2 * j + 1, j, 1, True)

            trp = [banks(0, 1)[:, 0:P], banks(1, 1)[:, 0:P]]

            def step4(p, j, i, first):
                par = i % 2
                wait_for(act, tr_ready, p + 1)
                wait_for(act, f_ready, 2 * (p - 1))
                act.activation(oe[par], trp[par], ACT.Copy, scale=inv[:, bass.ds(p, 1)]).then_inc(oe_done, 1)
                if first > 0:
                    store(p - 1, (i - 1) % RING)

            def store(p, i):
                wait_for(act, added, 2 * p + 2)
                act.dma_start(out_c[bass.ds(2 * p, 2), :, :].rearrange("b c s -> c b s"), x4[i]).then_inc(out_here[i], 16)

            run_phase4(act, step4)
            store(NP - 1, RING - 1)

        @block.vector
        def _(dve):
            psx = [banks(0, 2).rearrange("p (k c) -> p k c", k=NWB), banks(2, 2).rearrange("p (k c) -> p k c", k=NWB)]

            dve.memset(ones[:, :], 1.0).then_inc(ones_done, 1)
            dve.memset(neg_half[:, :], -0.5).then_inc(ones_done, 1)
            dve.wait_ge(p_here, 16)
            dve.transpose(p_cols, p_rows).then_inc(p_turned, 1)
            dve.wait_ge(ident_done, 2)
            dve.reduce_sum(col_mask[:, :], ident[:, :].rearrange("p (k q) -> p q k", q=WQ), AX.X).then_inc(p_turned, 1)
            dve.wait_ge(p_turned, 2)

            def spread_weights():
                for q in range(P // 16):
                    dve.wait_ge(pw_spread, q + 1)
                    dve.tensor_tensor(arena_w[:, q * 2048:q * 2048 + 2048].rearrange("p (m q) -> p m q", q=WQ),
                                      banks(4 + q % 4, 1).unsqueeze(2).to_broadcast((P, 512, WQ)),
                                      col_mask[:, :].unsqueeze(1).to_broadcast((P, 512, WQ)), ALU.mult).then_inc(pw_done, 1)
                dve.wait_ge(pw_done, P // 16)

            def image_stats(g, i):
                n = g * GB + i
                q = i % 2
                wait_for(dve, x_turned, n + 1)
                wait_for(dve, ln_rdone, n - 1)
                for k in range(0, NWB, 2):
                    last = dve.bn_stats(ln_st[q][:, k:k + 2, :].rearrange("p k t -> p (k t)"),
                                        psx[q][:, k:k + 2, :].rearrange("p k c -> p c k"))
                last.then_inc(ln_stats, 1)
                wait_for(dve, ln_stats, n + 1)
                wait_for(dve, ln_ndone, n - 1)
                dve.tensor_scalar(ln_neg[q][:, :], ln_st[q][:, :, 1], -1.0, None, ALU.mult).then_inc(ln_m, 1)
                dve.tensor_scalar(ln_var[q][:, :], ln_st[q][:, :, 2], 1.0 / P, EPS_C,
                                  ALU.mult, ALU.add).then_inc(ln_v, 1)

            def stage(gc, cp, gf, fp):
                if isinstance(gf, int) and gf == 0:
                    image_stats(0, 0)
                for i in range(GB):
                    ahead = image_ahead(gf, i, 1)
                    if ahead:
                        image_stats(*ahead)
                    if gc is not None:
                        wait_for(dve, v_done, gc * NCH + i + 1)
                        chunk = grp[cp][:, :, i * CH:i * CH + CH, :].rearrange("p b c w -> p b (c w)")
                        dve.scalar_tensor_tensor(out=chunk, in0=chunk, scalar=NEG_SLOPE, in1=chunk,
                                                 op0=ALU.mult, op1=ALU.max).then_inc(y_done, 1)
                    if gc is not None:
                        if i == 0 and not (isinstance(gc, int) and gc < 2):
                            wait_for(dve, y_acc, 3 * (gc - 1))
                        wait_for(dve, y_done, gc * NCH + i + 1)
                        for c in range(i * CH, i * CH + CH, 2):
                            last = dve.bn_stats(y_st[cp][:, c:c + 2, :].rearrange("p c t -> p (c t)"),
                                                grp[cp][:, :, c:c + 2, :].rearrange("p b c w -> p b w c"))
                        last.then_inc(y_stats, 1)

            run_phase1(dve, stage, spread_weights)

            n_part = GB * NWB
            dve.wait_ge(y_acc, 3 * G)
            dve.scalar_tensor_tensor(out=acc_sq[:, :], in0=acc_m2[:, :], scalar=1.0 / n_part, in1=acc_sq[:, :],
                                     op0=ALU.mult, op1=ALU.add).then_inc(bn_step, 1)
            dve.wait_ge(bn_sum, 1)
            dve.tensor_scalar(bn[:, 0:2], banks(0, 1)[:, 0:2], 1.0 / (P * G), None, ALU.mult).then_inc(bn_step, 1)
            dve.wait_ge(bn_step, 2)
            dve.tensor_tensor(bn[:, 2:3], bn[:, 0:1], bn[:, 0:1], ALU.mult).then_inc(bn_step, 1)
            dve.wait_ge(bn_step, 3)
            dve.tensor_tensor(bn[:, 3:4], bn[:, 1:2], bn[:, 2:3], ALU.subtract).then_inc(bn_step, 1)
            dve.wait_ge(bn_rs, 2)
            dve.tensor_tensor(bn_a, gamma_col[:, :], bn[:, 5:6], ALU.mult).then_inc(bn_step, 1)
            dve.wait_ge(bn_step, 5)
            dve.scalar_tensor_tensor(out=bn[:, 4:5], in0=bn[:, 0:1], scalar=bn_a, in1=beta_col[:, :],
                                     op0=ALU.mult, op1=ALU.subtract).then_inc(bn_rs, 1)
            dve.wait_ge(bn_rs, 3)
            dve.tensor_scalar(bn_b, bn[:, 4:5], -1.0, None, ALU.mult).then_inc(bn_step, 1)

            dve.wait_ge(gate_here, 48)
            dve.reduce_sum(gate_mean[0:E, 0:1], gate_rows[0:E, :], AX.X).then_inc(gate_step, 1)
            dve.wait_ge(gate_step, 1)
            dve.tensor_scalar(gate_mean[0:E, 1:2], gate_mean[0:E, 0:1], 1.0 / P, None, ALU.mult).then_inc(gate_step, 1)
            dve.wait_ge(gate_step, 2)
            dve.tensor_scalar(gate_cen[0:E, :], gate_rows[0:E, :], gate_mean[0:E, 1:2], None,
                              ALU.subtract).then_inc(gate_step, 1)
            dve.tensor_scalar(cmat, ident[:, :], -1.0 / P, None, ALU.add).then_inc(cmat_step, 1)

            pst = banks(2, 2).rearrange("p (m e) -> p m e", e=E)
            psm = banks(4, 2).rearrange("p (m e) -> p m e", e=E)
            pslt = banks(6, 2)

            def wide(r):
                return r.unsqueeze(2).to_broadcast((P, 16, E))

            def step(p, ph, quad, early, mid, late, last_):
                par, o = quad % 2, 1 - quad % 2

                def stats(q, b):
                    place = x1t_even[(quad + 1) % 4] if b == 0 else x1t_odd[par]
                    st = st2[b]
                    wait_for(dve, tx_copied, 2 * q + b + 1)
                    for k in range(0, 8, 2):
                        last = dve.bn_stats(st[:, k:k + 2, :].rearrange("p k t -> p (k t)"),
                                            place[:, k:k + 2, :].rearrange("p k c -> p c k"))
                    last.then_inc(tx_stats, 1)
                    wait_for(dve, tx_stats, 2 * q + b + 1)
                    wait_for(dve, r_ready, 2 * q + b - 1)
                    dve.tensor_scalar(var2[:, b, :], st[:, :, 2], 1.0 / P, EPS_T,
                                      ALU.mult, ALU.add).then_inc(v_ready, 1)

                if mid:
                    stats(p, 1)
                if late:
                    wait_for(dve, e8_done, p)
                    wait_for(dve, m_ready, p - 1)
                    dve.memset(small[:, 4:5], 0.0)
                    dve.match_replace(out=p0, in_to_replace=ex8, in_values=ex, imm_value=0.0).then_inc(match_done, 1)
                    wait_for(dve, match_done, p)
                    wait_for(dve, m_out[o], 16 * (ph - (1 - par)))
                    dve.tensor_tensor(mm_[o], ex, p0, ALU.subtract).then_inc(m_ready, 1)
                if mid:
                    wait_for(dve, l_ready, p + 1)
                    wait_for(dve, r_ready, 2 * p + 2)
                    wait_for(dve, lt_ready, p)
                    dve.tensor_tensor(ls.rearrange("p k (b e) -> p (k b) e", e=E), psm, wide(r2[par]), ALU.mult).then_inc(ls_done, 1)
                if late:
                    wait_for(dve, mt_ready, p)
                    wait_for(dve, pool_ready, p - 1)
                    dve.tensor_tensor(mt.rearrange("p k (b e) -> p (k b) e", e=E), pst, wide(r2[o]), ALU.mult).then_inc(mt_taken, 1)
                if mid:
                    wait_for(dve, lt_ready, p + 1)
                    wait_for(dve, e8_done, p)
                    dve.memset(small[:, 4:5], 0.0)
                    dve.max(mx8, pslt).then_inc(max_done, 1)
                    wait_for(dve, max_done, p + 1)
                    dve.tensor_tensor(small[:, 0:1], mx8[:, 0:1], gate_b_col[:, :], ALU.add).then_inc(nb_step, 1)
                    wait_for(dve, nb_step, p + 1)
                    dve.tensor_tensor(small[:, 1:2], gate_b_col[:, :], small[:, 0:1], ALU.subtract).then_inc(nb_ready, 1)
                    wait_for(dve, e_done, p + 1)
                    dve.reciprocal(inv[:, bass.ds(p, 1)], small[:, 2:3]).then_inc(inv_ready, 1)
                if early:
                    stats(p + 1, 0)

            dve.wait_ge(const_here, 16 * 5)
            dve.wait_ge(bn_step, 6)
            run_phase2(dve, step)

            psc = [banks(0, 1)[:, 0:B], banks(1, 1)[:, 0:B]]
            pso = [banks(6, 1)[:, 0:B], banks(7, 1)[:, 0:B]]

            def take_centred(e, ep):
                wait_for(dve, c_ready, e + 1)
                wait_for(dve, h_ready, HC * (e - 1))
                dve.tensor_copy(pc[ep], psc[ep]).then_inc(pc_done, 1)

            def expert(e, eh, ep, more):
                if more:
                    take_centred(e + 1, 1 - ep)
                wait_for(dve, o_ready, e + 1)
                dve.tensor_scalar(pooled[:, :, e], pso[ep], b2t[:, bass.ds(e, 1)], None, ALU.add).then_inc(o_taken, 1)

            dve.wait_ge(small_copied, 3)
            take_centred(0, 0)
            run_phase3(dve, expert)

            psf = banks(4, 4).rearrange("p (b s) -> p b s", b=2)

            def step4(p, j, i, first):
                wait_for(dve, l4_here[i], 32 * (j + 1))
                for b in range(2):
                    wait_for(dve, f_ready, 2 * p + b + 1)
                    dve.tensor_tensor(x4[i][:, b, :], psf[:, b, :], x4[i][:, b, :], ALU.add).then_inc(added, 1)

            run_phase4(dve, step4)

        @block.gpsimd
        def _(pool):
            pool.memset(ident[:, :], 0.0).then_inc(ident_done, 1)
            pool.wait_ge(ident_done, 1)
            pool.affine_select(out=ident[:, :], in_=ident[:, :], compare_op=ALU.not_equal, fill=1.0,
                               base=0, pattern=[[-1, P]], channel_multiplier=1).then_inc(ident_done, 1)
            pool.memset(spread[:, :], 0.0).then_inc(spread_done, 1)
            pool.wait_ge(spread_done, 1)
            sv = spread[:, :].rearrange("h (k q) -> h k q", q=WQ)
            pool.affine_select(out=sv, in_=sv, compare_op=ALU.not_equal, fill=1.0,
                               base=0, pattern=[[-1, S], [0, WQ]], channel_multiplier=1).then_inc(spread_done, 1)
            for a in (acc_mean, acc_m2, acc_sq):
                pool.memset(a[:, :], 0.0).then_inc(y_sq, 1)

            def image_r(g, i):
                n = g * GB + i
                q = i % 2
                wait_for(pool, ln_v, n + 1)
                wait_for(pool, norm_act, n - 1)
                pool.tensor_tensor(ln_r[q][:, :], ln_var[q][:, :], neg_half[:, 0:NWB], ALU.pow).then_inc(ln_rdone, 1)
                wait_for(pool, ln_m, n + 1)
                wait_for(pool, ln_rdone, n + 1)
                pool.tensor_tensor(ln_nmr[q][:, :], ln_neg[q][:, :], ln_r[q][:, :], ALU.mult).then_inc(ln_ndone, 1)

            def stage(gc, cp, gf, fp):
                if isinstance(gf, int) and gf == 0:
                    image_r(0, 0)
                for i in range(GB):
                    if image_ahead(gf, i, 1):
                        image_r(*image_ahead(gf, i, 1))
                if gc is not None:
                    wait_for(pool, y_stats, NCH * gc + NCH)
                    wait_for(pool, y_acc, 3 * gc)
                    mean = y_st[cp][:, :, 1]
                    pool.tensor_tensor(sq[:, :], mean, mean, ALU.mult).then_inc(y_sq, 1)
                    pool.tensor_tensor(acc_mean[:, :], acc_mean[:, :], mean, ALU.add).then_inc(y_acc, 1)
                    pool.tensor_tensor(acc_m2[:, :], acc_m2[:, :], y_st[cp][:, :, 2], ALU.add).then_inc(y_acc, 1)
                    wait_for(pool, y_sq, gc + 4)
                    pool.tensor_tensor(acc_sq[:, :], acc_sq[:, :], sq[:, :], ALU.add).then_inc(y_acc, 1)

            pool.wait_ge(ones_done, 2)
            pool.wait_ge(y_sq, 3)
            run_phase1(pool, stage)

            pool.wait_ge(bn_step, 4)
            pool.tensor_scalar(bn[:, 4:5], bn[:, 3:4], EPS_BN, None, ALU.add).then_inc(bn_rs, 1)
            pool.wait_ge(bn_rs, 1)
            pool.tensor_tensor(bn[:, 5:6], bn[:, 4:5], neg_half[:, 0:1], ALU.pow).then_inc(bn_rs, 1)

            def step(p, ph, quad, early, mid, late, last_):
                par, o = quad % 2, 1 - quad % 2
                def rstd(q, b, place):
                    wait_for(pool, mt_taken, q - 1)
                    wait_for(pool, ls_done, q - 1)
                    wait_for(pool, v_ready, 2 * q + b + 1)
                    pool.tensor_tensor(place.rearrange("p (k b) -> p b k", b=2)[:, b, :], var2[:, b, :],
                                       neg_half[:, 0:8], ALU.pow).then_inc(r_ready, 1)

                if mid:
                    rstd(p, 1, r2[par])
                if early:
                    wait_for(pool, xb_here[o], 16 * (ph + par + 1))
                    wait_for(pool, x1_out[o], 16 * (ph + par))
                    wait_for(pool, l_ready, p)
                    for b in range(2):
                        wait_for(pool, t_ready, 2 * p + 3 + b)
                        pool.tensor_tensor(x1[o][:, b, :].rearrange("p (m k) -> p m k", k=NWB),
                                           tb[b].rearrange("p (k m) -> p m k", k=NWB),
                                           xb[o][:, b, :].rearrange("p (m k) -> p m k", k=NWB),
                                           ALU.add).then_inc(x1_sum, 1)
                    rstd(p + 1, 0, r2[o])

            run_phase2(pool, step)

            pool.wait_ge(o_taken, E)

            def step4(p, j, i, first):
                par = i % 2
                wait_for(pool, tr_ready, p - 1)
                pool.tensor_copy(stg[par], pooled[:, bass.ds(2 * p, 2), :].rearrange("p b e -> p (b e)")).then_inc(stg_done, 1)

            run_phase4(pool, step4)


_INS = ['x', 'L0_conv_P', 'L0_conv_lam', 'L0_conv_gamma', 'L0_conv_beta', 'L0_ffn_gate_w', 'L0_ffn_gate_b',
        'L0_ffn_weight1', 'L0_ffn_weight2']


def kernel(**inputs):
    import numpy as _np
    import concourse.bacc as _bacc
    from concourse import mybir as _mybir
    from concourse.bass_utils import run_bass_kernel_spmd as _run

    nc = _bacc.Bacc("TRN2", target_bir_lowering=False, num_devices=1)
    arrays, args = {}, []
    for name in _INS:
        a = _np.ascontiguousarray(inputs[name])
        arrays[f"in_{name}_dram"] = a
        args.append(nc.dram_tensor(f"in_{name}_dram", a.shape, _mybir.dt.from_np(a.dtype), kind="ExternalInput").ap())
    shape = inputs['x'].shape
    args.append(nc.dram_tensor("out_0_dram", tuple(shape), _mybir.dt.float32, kind="ExternalOutput").ap())
    metaformer_kernel(nc, *args)
    r = _run(nc, [arrays], core_ids=[0])
    return r.results[0]["out_0_dram"]
```

```python
from contextlib import ExitStack

import concourse.bass as bass
from concourse import mybir

F32 = mybir.dt.float32
ALU = mybir.AluOpType
ACT = mybir.ActivationFunctionType
AX = mybir.AxisListType

P = 128
HW = 1024
S = 32
NWB = 8
WQ = 4
GB = 16
CH = 8
NCH = P // CH
E = 64
K8 = 8
HID = 512
HC = HID // P
NEG_SLOPE = 0.2
EPS_C, EPS_BN, EPS_T = 1e-6, 1e-5, 1e-5
RING = 4
assert NCH == GB


def wait_for(eng, semaphore, count):
    if isinstance(count, int) and count <= 0:
        return
    eng.wait_ge(semaphore, count)


def metaformer_kernel(nc, x, conv_p, lam, gamma, beta, gate_w, gate_b, weight1, weight2, out):
    B = x.shape[0]
    G = B // GB
    NP = B // 2
    assert G % 2 == 0 and G >= 6 and NP % RING == 0

    x_c = x.rearrange("b c h w -> b c (h w)")
    out_c = out.rearrange("b c h w -> b c (h w)")

    y_dram = nc.dram_tensor("y_scratch", (B, P, HW), F32, kind="Internal").ap()
    x1_dram = nc.dram_tensor("x1_scratch", (B, P, HW), F32, kind="Internal").ap()
    m_dram = nc.dram_tensor("m_scratch", (NP, P, HW), F32, kind="Internal").ap()

    with ExitStack() as ctx:
        def sb(name, shape):
            return ctx.enter_context(nc.sbuf_tensor(name, shape, F32))

        def sem(name):
            return ctx.enter_context(nc.semaphore(name))

        arena_w = sb("arena_w", [P, P * P])
        pw = arena_w[:, :].rearrange("p (c m) -> p c m", c=P)
        pooled = arena_w[:, 0:B * E].rearrange("p (b e) -> p b e", e=E)
        arena_g = sb("arena_g", [P, 2 * GB * HW])
        grp = [arena_g[:, i * GB * HW:(i + 1) * GB * HW].rearrange("p (b c w) -> p b c w", b=GB, c=P)
               for i in range(2)]
        cursor = [0]

        def carve(n):
            a = cursor[0]
            cursor[0] += n
            assert cursor[0] <= 2 * GB * HW
            return arena_g[:, a:a + n]

        p_rows = arena_g[0:S, GB * HW:GB * HW + P * S]
        p_cols = arena_g[0:S, GB * HW + P * S:GB * HW + 2 * P * S]
        xin = [sb(f"xin{i}", [P, HW]) for i in range(2)]
        gate_rows = xin[0][:, 0:P]
        b2_rows = xin[0][:, P:2 * P]
        b1_rows = xin[1][:, 0:HID]
        spread = sb("spread", [S, P])
        col_mask = sb("col_mask", [P, WQ])
        ident = sb("ident", [P, P])
        ones = sb("ones", [P, 1])
        neg_half = sb("neg_half", [P, 16])
        lam_col = sb("lam_col", [P, 1])
        gamma_col = sb("gamma_col", [P, 1])
        beta_col = sb("beta_col", [P, 1])
        gate_b_col = sb("gate_b_col", [P, 1])
        ln_st = [sb(f"ln_st{i}", [P, NWB, 3]) for i in range(2)]
        ln_var = [sb(f"ln_var{i}", [P, NWB]) for i in range(2)]
        ln_r = [sb(f"ln_r{i}", [P, NWB]) for i in range(2)]
        ln_neg = [sb(f"ln_neg{i}", [P, NWB]) for i in range(2)]
        ln_nmr = [sb(f"ln_nmr{i}", [P, NWB]) for i in range(2)]
        y_st = [sb(f"y_st{i}", [P, P, 3]) for i in range(2)]
        acc_mean = sb("acc_mean", [P, P])
        acc_m2 = sb("acc_m2", [P, P])
        acc_sq = sb("acc_sq", [P, P])
        sq = sb("sq", [P, P])
        bn = sb("bn", [P, 8])
        inv = sb("inv", [P, NP])
        bn_a, bn_b = bn[:, 6:7], bn[:, 7:8]

        xb = [carve(2 * HW).rearrange("p (b s) -> p b s", b=2) for _ in range(2)]
        yb = [carve(2 * HW).rearrange("p (b c w) -> p b c w", b=2, c=P) for _ in range(2)]
        x1 = [carve(2 * HW).rearrange("p (b s) -> p b s", b=2) for _ in range(2)]
        tb = [carve(HW) for _ in range(2)]
        gate_cen = carve(P)
        gate_mean = carve(8)
        gwt = carve(E)
        b1t = carve(HC * E).rearrange("p (k e) -> p k e", k=HC)
        b2t = carve(E)
        x1t_odd = [carve(HW).rearrange("p (k c) -> p k c", k=8)]
        assert cursor[0] <= GB * HW
        cursor[0] = GB * HW
        x1t_odd += [carve(HW).rearrange("p (k c) -> p k c", k=8) for _ in range(3)]
        x1t_even = [carve(HW).rearrange("p (k c) -> p k c", k=8) for _ in range(4)]
        ls = carve(HW).rearrange("p (k m) -> p k m", k=8)
        ex = carve(HW)
        p0 = carve(HW)
        mm_ = [carve(HW) for _ in range(2)]
        mt = carve(HW).rearrange("p (k m) -> p k m", k=8)
        pl = carve(P)
        pl_raw = carve(P)
        pl_sum = carve(8)
        mx8 = carve(K8)
        ex8 = carve(K8)
        small = carve(8)
        st2 = [carve(24).rearrange("p (k t) -> p k t", k=8) for _ in range(2)]
        var2 = carve(16).rearrange("p (b k) -> p b k", b=2)
        r2 = [carve(16) for _ in range(2)]
        w_buf = [carve(HID + HC * P) for _ in range(2)] + [t.rearrange("p k c -> p (k c)") for t in x1t_odd[2:]]
        w1 = [w[:, 0:HID] for w in w_buf]
        w2 = [w[:, HID:HID + HC * P].rearrange("p (k o) -> p k o", k=HC) for w in w_buf]
        hb = [tb[i][:, 0:HC * B].rearrange("p (k b) -> p k b", k=HC) for i in range(2)]
        cursor[0] = 0
        x4 = [carve(2 * HW).rearrange("p (b s) -> p b s", b=2) for _ in range(RING)]
        m4 = [carve(HW) for _ in range(RING)]
        stg = [carve(P) for _ in range(2)]
        oe = [carve(P) for _ in range(2)]

        ps = ctx.enter_context(nc.psum_tensor("ps", [P, 8 * 512], F32))

        def banks(a, n):
            return ps[:, a * 512:(a + n) * 512]

        const_here = sem("const_here")
        p_here = sem("p_here")
        p_turned = sem("p_turned")
        spread_done = sem("spread_done")
        pw_spread = sem("pw_spread")
        pw_done = sem("pw_done")
        ident_done = sem("ident_done")
        ones_done = sem("ones_done")
        x_here = [sem(f"x_here{i}") for i in range(2)]
        x_half = sem("x_half")
        x_turned = sem("x_turned")
        ln_stats = sem("ln_stats")
        ln_m = sem("ln_m")
        ln_v = sem("ln_v")
        ln_rdone = sem("ln_rdone")
        ln_ndone = sem("ln_ndone")
        norm_act = sem("norm_act")
        z_ready = sem("z_ready")
        v_done = sem("v_done")
        y_done = sem("y_done")
        y_stats = sem("y_stats")
        y_sq = sem("y_sq")
        y_acc = sem("y_acc")
        y_out = [sem(f"y_out{i}") for i in range(4)]
        last_out = sem("last_out")

        bn_step = sem("bn_step")
        bn_sum = sem("bn_sum")
        bn_rs = sem("bn_rs")
        gate_here = sem("gate_here")
        gate_step = sem("gate_step")
        turned_small = sem("turned_small")
        small_copied = sem("small_copied")

        xb_here = [sem(f"xb_here{i}") for i in range(2)]
        yb_here = [sem(f"yb_here{i}") for i in range(2)]
        x1_out = [sem(f"x1_out{i}") for i in range(2)]
        m_out = [sem(f"m_out{i}") for i in range(2)]
        ty_ready = sem("ty_ready")
        t_ready = sem("t_ready")
        x1_sum = sem("x1_sum")
        tx_ready = sem("tx_ready")
        tx_copied = sem("tx_copied")
        tx_stats = sem("tx_stats")
        v_ready = sem("v_ready")
        r_ready = sem("r_ready")
        l_ready = sem("l_ready")
        ls_done = sem("ls_done")
        lt_ready = sem("lt_ready")
        max_done = sem("max_done")
        nb_step = sem("nb_step")
        nb_ready = sem("nb_ready")
        e_done = sem("e_done")
        e8_done = sem("e8_done")
        inv_ready = sem("inv_ready")
        match_done = sem("match_done")
        m_ready = sem("m_ready")
        mt_ready = sem("mt_ready")
        mt_taken = sem("mt_taken")
        pool_ready = sem("pool_ready")
        pl_step = sem("pl_step")
        pl_done = sem("pl_done")
        pt_ready = sem("pt_ready")
        pt_taken = sem("pt_taken")

        w_here = [sem(f"w_here{i}") for i in range(4)]
        h_ready = sem("h_ready")
        g_ready = sem("g_ready")
        o_ready = sem("o_ready")
        o_taken = sem("o_taken")

        l4_here = [sem(f"l4_here{i}") for i in range(RING)]
        out_here = [sem(f"out_here{i}") for i in range(RING)]
        stg_done = sem("stg_done")
        tr_ready = sem("tr_ready")
        oe_done = sem("oe_done")
        f_ready = sem("f_ready")
        added = sem("added")

        block = ctx.enter_context(nc.Block())

        def run_phase1(eng, stage):
            stage(None, 0, 0, 0)
            stage(0, 0, 1, 1)
            stage(1, 1, 2, 0)
            with eng.Fori(1, G // 2 - 1) as j:
                stage(2 * j, 0, 2 * j + 1, 1)
                stage(2 * j + 1, 1, 2 * j + 2, 0)
            stage(G - 2, 0, G - 1, 1)
            stage(G - 1, 1, None, 0)

        def image_ahead(g, i, d):
            if g is None:
                return None
            if i + d < GB:
                return g, i + d
            return None if isinstance(g, int) and g == G - 1 else (g + 1, i + d - GB)

        def run_phase2(eng, step):
            step(-1, -1, 3, early=True, mid=False, late=False, last_=False)
            step(0, 0, 0, early=True, mid=True, late=False, last_=False)
            step(1, 0, 1, early=True, mid=True, late=True, last_=False)
            step(2, 1, 2, early=True, mid=True, late=True, last_=True)
            with eng.Fori(1, NP // 4) as j:
                step(4 * j - 1, 2 * j - 1, 3, early=True, mid=True, late=True, last_=True)
                step(4 * j, 2 * j, 0, early=True, mid=True, late=True, last_=True)
                step(4 * j + 1, 2 * j, 1, early=True, mid=True, late=True, last_=True)
                step(4 * j + 2, 2 * j + 1, 2, early=True, mid=True, late=True, last_=True)
            step(NP - 1, NP // 2 - 1, 3, early=False, mid=True, late=True, last_=True)
            step(NP, NP // 2, 0, early=False, mid=False, late=True, last_=True)
            step(NP + 1, NP // 2, 1, early=False, mid=False, late=False, last_=True)

        def run_phase3(eng, step):
            for i in range(4):
                step(i, 0, i, True)
            with eng.Fori(1, E // 4 - 1) as j:
                for i in range(4):
                    step(4 * j + i, j, i, True)
            for i in range(4):
                step(E - 4 + i, E // 4 - 1, i, i < 3)

        def run_phase4(eng, step):
            for i in range(RING):
                step(i, 0, i, i)
            with eng.Fori(1, NP // RING) as j:
                for i in range(RING):
                    step(RING * j + i, j, i, RING + i)

        @block.sync
        def _(sp):
            sp.dma_start(p_rows.rearrange("k (c h) -> k c h", c=P), conv_p.rearrange("c k h -> k c h")).then_inc(p_here, 16)
            sp.dma_start(lam_col[:, :], lam.rearrange("(a n) -> a n", a=1).to_broadcast((P, 1))).then_inc(const_here, 16)
            sp.dma_start(gamma_col[:, :], gamma.rearrange("(p a) -> p a", a=1)).then_inc(const_here, 16)
            sp.dma_start(beta_col[:, :], beta.rearrange("(p a) -> p a", a=1)).then_inc(const_here, 16)
            for i in range(2):
                sp.dma_start(gate_b_col[E * i:E * i + E, :],
                             gate_b.rearrange("(p a) -> p a", a=1)).then_inc(const_here, 16)

            def store_y(g, gp, i):
                if i == 0:
                    wait_for(sp, y_done, NCH * g + NCH)
                wait_for(sp, y_out[i % 4], 16 * (g * (GB // 4) + i // 4))
                sp.dma_start(y_dram[g * GB + i, :, :].unsqueeze(0).rearrange("a p s -> p (a s)"),
                             grp[gp][:, i, :, :].rearrange("p c w -> p (c w)")).then_inc(y_out[i % 4], 16)

            def load_x(g, i):
                wait_for(sp, x_turned, g * GB + i - 1)
                sp.dma_start(xin[i % 2][:, :], x_c[g * GB + i, :, :]).then_inc(x_here[i % 2], 16)

            def stage(gc, cp, gf, fp):
                if isinstance(gf, int) and gf == 0:
                    load_x(0, 0)
                    load_x(0, 1)
                for i in range(GB):
                    if image_ahead(gf, i, 2):
                        load_x(*image_ahead(gf, i, 2))
                    if gc is not None and not (isinstance(gc, int) and gc == 0):
                        store_y(gc - 1, 1 - cp, i)

            run_phase1(sp, stage)

            wait_for(sp, x_turned, B)
            sp.dma_start(gate_rows[0:E, :], gate_w).then_inc(gate_here, 16)
            sp.dma_start(b1_rows[0:E, :], weight1[:, P, :]).then_inc(gate_here, 16)
            sp.dma_start(b2_rows[0:E, :], weight2[:, HID, :]).then_inc(gate_here, 16)

            def load(q, qp):
                wait_for(sp, x1_sum, 2 * q - 2)
                wait_for(sp, ty_ready, 2 * q - 2)
                sp.dma_start(xb[qp], x_c[bass.ds(2 * q, 2), :, :].rearrange("b c s -> c b s")).then_inc(xb_here[qp], 16)
                sp.dma_start(yb[qp].rearrange("p b c w -> p b (c w)"),
                             y_dram[bass.ds(2 * q, 2), :, :].rearrange("b p s -> p b s")).then_inc(yb_here[qp], 16)

            def store_x1(q, qp):
                wait_for(sp, x1_sum, 2 * q + 2)
                sp.dma_start(x1_dram[bass.ds(2 * q, 2), :, :].rearrange("b c s -> c b s"), x1[qp]).then_inc(x1_out[qp], 16)

            def store_m(q, qp):
                wait_for(sp, m_ready, q + 1)
                sp.dma_start(m_dram[q, :, :], mm_[qp]).then_inc(m_out[qp], 16)

            for i in range(4):
                wait_for(sp, y_out[i], 16 * ((G - 1) * (GB // 4)))
            wait_for(sp, y_stats, NCH * (G - 1))
            load(0, 0)
            load(1, 1)
            for h in range(2):
                wait_for(sp, y_done, NCH * (G - 1) + (h + 1) * NCH // 2)
                for i in range(4):
                    sp.dma_start(y_dram[(G - 1) * GB + 4 * i:(G - 1) * GB + 4 * i + 4, :,
                                        h * HW // 2:(h + 1) * HW // 2].rearrange("b p s -> p b s"),
                                 grp[1][:, 4 * i:4 * i + 4, h * P // 2:(h + 1) * P // 2, :]
                                 .rearrange("p b c w -> p b (c w)")).then_inc(last_out, 16)

            for q in range(4):
                if q >= 2:
                    load(q, q % 2)
                if q >= 1:
                    store_x1(q - 1, (q - 1) % 2)
                if q >= 3:
                    store_m(q - 3, (q - 3) % 2)
            wait_for(sp, last_out, 16 * 8)
            with sp.Fori(2, NP // 2) as j:
                for i in range(2):
                    load(2 * j + i, i)
                    store_x1(2 * j + i - 1, 1 - i)
                    store_m(2 * j + i - 3, 1 - i)
            store_x1(NP - 1, 1)
            for q in range(NP - 3, NP):
                store_m(q, q % 2)

            def load_w(e, ep):
                wait_for(sp, h_ready, HC * (e - 3))
                wait_for(sp, o_ready, e - 3)
                sp.dma_start(w1[ep], weight1[e, 0:P, :]).then_inc(w_here[ep], 16)
                sp.dma_start(w2[ep], weight2[e, 0:HID, :].rearrange("(k p) o -> p k o", p=P)).then_inc(w_here[ep], 16)

            def load4(p, j, i):
                wait_for(sp, out_here[i], 16 * j)
                sp.dma_start(x4[i], x1_dram[bass.ds(2 * p, 2), :, :].rearrange("b c s -> c b s")).then_inc(l4_here[i], 16)
                sp.dma_start(m4[i], m_dram[p, :, :]).then_inc(l4_here[i], 16)

            load_w(0, 0)
            load_w(1, 1)
            for i in range(2):
                wait_for(sp, x1_out[i], 16 * (NP // 2))
                wait_for(sp, m_out[i], 16 * (NP // 2))
            wait_for(sp, pt_taken, NP)
            load_w(2, 2)
            load_w(3, 3)
            for i in range(RING):
                load4(i, 0, i)
            with sp.Fori(1, E // 4) as j:
                for i in range(4):
                    load_w(4 * j + i, i)
            with sp.Fori(1, NP // RING) as j:
                for i in range(RING):
                    load4(RING * j + i, j, i)
            for i in range(RING):
                wait_for(sp, out_here[i], 16 * (NP // RING))

        @block.tensor
        def _(pe):
            psx = [banks(0, 2).rearrange("p (k c) -> p k c", k=NWB), banks(2, 2).rearrange("p (k c) -> p k c", k=NWB)]
            psz = [banks(4, 2).rearrange("p (c n) -> p c n", c=CH), banks(6, 2).rearrange("p (c n) -> p c n", c=CH)]

            def turn_image(g, i):
                n = g * GB + i
                wait_for(pe, x_here[i % 2], 16 * (g * (GB // 2) + i // 2 + 1))
                for half in range(2):
                    wait_for(pe, norm_act, 2 * n - 3 + half)
                    for k in range(half * NWB // 2, (half + 1) * NWB // 2):
                        last = pe.transpose(psx[i % 2][:, k, :], xin[i % 2][:, k:HW:NWB], ident[:, :])
                    last.then_inc((x_half, x_turned)[half], 1)

            def conv_chunk(g, gp, i):
                m = g * NCH + i
                if i == 0:
                    wait_for(pe, norm_act, 2 * (GB * g + GB))
                wait_for(pe, v_done, m - 1)
                for c in range(CH):
                    last = pe.matmul(psz[i % 2][:, c, :], pw[:, i * CH + c, :], grp[gp][:, :, i * CH + c, :],
                                     start=True, stop=True)
                last.then_inc(z_ready, 1)

            def stage(gc, cp, gf, fp):
                if isinstance(gf, int) and gf == 0:
                    turn_image(0, 0)
                    pe.wait_ge(spread_done, 2)
                    pe.wait_ge(p_turned, 1)
                for i in range(GB):
                    if image_ahead(gf, i, 1):
                        turn_image(*image_ahead(gf, i, 1))
                    if gc is None and i % 2 == 0:
                        q = i // 2
                        wait_for(pe, pw_done, q - 3)
                        pe.matmul(banks(4 + q % 4, 1), spread[:, :], p_cols[:, q * 512:q * 512 + 512],
                                  start=True, stop=True).then_inc(pw_spread, 1)
                    if gc is not None:
                        if i == 0 and isinstance(gc, int) and gc == 0:
                            pe.wait_ge(pw_done, P // 16)
                        conv_chunk(gc, cp, i)

            pe.wait_ge(ident_done, 2)

            run_phase1(pe, stage)

            pe.wait_ge(gate_step, 3)
            pe.wait_ge(gate_here, 48)
            pe.transpose(banks(2, 1)[:, 0:E], gate_cen[0:E, :], ident[0:E, 0:E])
            for k in range(HC):
                pe.transpose(banks(3, 1)[:, k * E:k * E + E], b1_rows[0:E, k * P:k * P + P], ident[0:E, 0:E])
            pe.transpose(banks(2, 1)[:, E:2 * E], b2_rows[0:E, :], ident[0:E, 0:E]).then_inc(turned_small, 1)
            pe.wait_ge(bn_step, 1)
            pe.wait_ge(y_acc, 3 * G)
            pe.wait_ge(ones_done, 1)
            pe.matmul(banks(0, 1)[:, 0:1], acc_mean[:, :], ones[:, :], start=True, stop=True)
            pe.matmul(banks(0, 1)[:, 1:2], acc_sq[:, :], ones[:, :], start=True, stop=True).then_inc(bn_sum, 1)
            pe.wait_ge(small_copied, 3)
            pe.wait_ge(bn_step, 2)

            psy = banks(0, 2)
            pst = banks(2, 2).rearrange("p (k c) -> p k c", k=8)
            psm = banks(4, 2).rearrange("p (k m) -> p k m", k=8)
            pslt = banks(6, 2)

            def step(p, ph, quad, early, mid, late, last_):
                par, o = quad % 2, 1 - quad % 2

                def turn_x1(q, x1_q, b):
                    wait_for(pe, x1_sum, 2 * q + b + 1)
                    wait_for(pe, tx_copied, 2 * q + b)
                    for k in range(8):
                        last = pe.transpose(pst[:, k, :], x1_q[:, b, k * P:k * P + P], ident[:, :])
                    last.then_inc(tx_ready, 1)

                def turn_y(b):
                    if b == 0:
                        wait_for(pe, yb_here[o], 16 * (ph + par + 1))
                        wait_for(pe, pl_done, p - 1)
                    wait_for(pe, t_ready, 2 * p + 2 + b)
                    for k in range(NWB):
                        last = pe.transpose(psy[:, k * P:k * P + P], yb[o][:, b, :, k], ident[:, :])
                    last.then_inc(ty_ready, 1)

                def logits(b):
                    wait_for(pe, ls_done, p)
                    for k in range(8):
                        for h in range(0, P, E):
                            last = pe.matmul(psm[h:h + E, k, b * E:b * E + E],
                                             x1[par][:, b, k * P + h:k * P + h + E], gwt, start=True, stop=True)
                    if b == 1:
                        last.then_inc(l_ready, 1)

                if mid:
                    logits(0)
                if early:
                    turn_y(0)
                if mid:
                    logits(1)
                if last_:
                    wait_for(pe, pl_done, p - 1)
                    wait_for(pe, mt_taken, p - 1)
                    wait_for(pe, tx_copied, 2 * p + 2 if mid else 2 * NP)
                    pe.transpose(pst[:, 0, :], pl, ident[:, :]).then_inc(pt_ready, 1)
                if early:
                    turn_y(1)
                if late:
                    wait_for(pe, m_ready, p)
                    wait_for(pe, tx_copied, 2 * p + 2 if mid else 2 * NP)
                    wait_for(pe, pt_taken, p - 1)
                    for k in range(8):
                        last = pe.transpose(pst[:, k, :], mm_[o][:, k * P:k * P + P], ident[:, :])
                    last.then_inc(mt_ready, 1)
                if mid:
                    wait_for(pe, ls_done, p + 1)
                    wait_for(pe, e_done, p)
                    for k in range(8):
                        last = pe.transpose(pslt[:, k * P:k * P + P], ls[:, k, :], ident[:, :])
                    last.then_inc(lt_ready, 1)
                if early:
                    wait_for(pe, mt_taken, p)
                    turn_x1(p + 1, x1[o], 0)
                if late:
                    wait_for(pe, mt_taken, p)
                    wait_for(pe, t_ready, 2 * p + 4 if early else 2 * NP)
                    wait_for(pe, pl_done, p - 1)
                    for k in range(8):
                        if early and k == 4:
                            turn_x1(p + 1, x1[o], 1)
                        for b, x1t in ((0, x1t_even[(quad - 1) % 4]), (1, x1t_odd[(quad - 1) % 4])):
                            last = pe.matmul(psy[b * E:b * E + E, 0:P], mt[:, k, b * E:b * E + E], x1t[:, k, :],
                                             start=(k == 0), stop=(k == 7))
                    last.then_inc(pool_ready, 1)
                elif early:
                    turn_x1(p + 1, x1[o], 1)

            run_phase2(pe, step)

            psh = [banks(2, 2).rearrange("p (k b) -> p k b", k=HC), banks(4, 2).rearrange("p (k b) -> p k b", k=HC)]
            pso = [banks(6, 1)[:, 0:B], banks(7, 1)[:, 0:B]]

            def hidden(e, j, i):
                wait_for(pe, w_here[i], 32 * (j + 1))
                wait_for(pe, g_ready, HC * (e - 1))
                for k in range(HC):
                    pe.matmul(psh[i % 2][:, k, 0:B], w1[i][:, k * P:k * P + P], pooled[:, :, e],
                              start=True, stop=True).then_inc(h_ready, 1)

            def expert(e, j, i, more):
                if more:
                    hidden(e + 1, j + (i + 1) // 4, (i + 1) % 4)
                wait_for(pe, o_taken, e - 1)
                for k in range(HC):
                    wait_for(pe, g_ready, HC * e + k + 1)
                    last = pe.matmul(pso[i % 2], w2[i][:, k, :], hb[i % 2][:, k, :], start=(k == 0), stop=(k == HC - 1))
                last.then_inc(o_ready, 1)

            pe.wait_ge(pt_taken, NP)
            hidden(0, 0, 0)
            run_phase3(pe, expert)

            trp = [banks(0, 1)[:, 0:P], banks(1, 1)[:, 0:P]]
            psf = banks(4, 4).rearrange("p (b s) -> p b s", b=2)

            def turn_out(p, par):
                wait_for(pe, stg_done, p + 1)
                wait_for(pe, oe_done, p - 1)
                pe.transpose(trp[par], stg[par], ident[:, :]).then_inc(tr_ready, 1)

            def step4(p, j, i, more):
                par = i % 2
                if more:
                    turn_out(p + 1, 1 - par)
                wait_for(pe, l4_here[i], 32 * (j + 1))
                wait_for(pe, oe_done, p + 1)
                for b in range(2):
                    wait_for(pe, added, 2 * p + b - 1)
                    for h in range(2):
                        last = pe.matmul(psf[:, b, h * 512:h * 512 + 512], oe[par][b * E:b * E + E, :],
                                         m4[i][b * E:b * E + E, h * 512:h * 512 + 512], start=True, stop=True)
                    last.then_inc(f_ready, 1)

            turn_out(0, 0)
            for i in range(RING):
                step4(i, 0, i, True)
            with pe.Fori(1, NP // RING - 1) as j:
                for i in range(RING):
                    step4(RING * j + i, j, i, True)
            for i in range(RING):
                step4(NP - RING + i, NP // RING - 1, i, i < RING - 1)

        @block.scalar
        def _(act):
            psx = [banks(0, 2).rearrange("p (k c) -> p k c", k=NWB), banks(2, 2).rearrange("p (k c) -> p k c", k=NWB)]
            psz = [banks(4, 2).rearrange("p (c b w) -> p c b w", c=CH, b=GB),
                   banks(6, 2).rearrange("p (c b w) -> p c b w", c=CH, b=GB)]

            def stage(gc, cp, gf, fp):
                def normalised(i):
                    n = gf * GB + i
                    wait_for(act, ln_ndone, n + 1)
                    if not (isinstance(gf, int) and gf < 2):
                        if i == 0:
                            wait_for(act, y_stats, NCH * (gf - 2) + NCH)
                        wait_for(act, y_out[i % 4], 16 * ((gf - 2) * (GB // 4) + i // 4 + 1))
                    for half in range(2):
                        for k in range(half * NWB // 2, (half + 1) * NWB // 2):
                            last = act.activation(grp[fp][:, i, :, k], psx[i % 2][:, k, :], ACT.Identity,
                                                  bias=ln_nmr[i % 2][:, k:k + 1], scale=ln_r[i % 2][:, k:k + 1])
                        last.then_inc(norm_act, 1)

                def scaled(i):
                    wait_for(act, z_ready, gc * NCH + i + 1)
                    act.activation(grp[cp][:, :, i * CH:i * CH + CH, :].rearrange("p b c w -> p c b w"),
                                   psz[i % 2], ACT.Copy, scale=lam_col[:, :]).then_inc(v_done, 1)

                if isinstance(gf, int) and gf == 1:
                    act.wait_ge(pw_done, P // 16)
                for i in range(GB):
                    if gf is not None:
                        normalised(i)
                    if gc is not None:
                        scaled(i)

            act.wait_ge(const_here, 16 * 5)
            run_phase1(act, stage)

            act.wait_ge(turned_small, 1)
            act.activation(gwt, banks(2, 1)[:, 0:E], ACT.Copy).then_inc(small_copied, 1)
            act.activation(b1t.rearrange("p k e -> p (k e)"), banks(3, 1)[:, 0:HC * E], ACT.Copy).then_inc(small_copied, 1)
            act.activation(b2t, banks(2, 1)[:, E:2 * E], ACT.Copy).then_inc(small_copied, 1)

            psy = banks(0, 2)
            pst = banks(2, 2)
            pslt = banks(6, 2)

            def step(p, ph, quad, early, mid, late, last_):
                par, o = quad % 2, 1 - quad % 2

                def scaled_y(b):
                    wait_for(act, ty_ready, 2 * p + 3 + b)
                    wait_for(act, x1_sum, 2 * p + b + 1)
                    act.activation(tb[b], psy, ACT.Identity, bias=bn_b, scale=bn_a).then_inc(t_ready, 1)

                def copy_x1(q, b):
                    if isinstance(q, int) and q == 0 and b == 0:
                        act.wait_ge(last_out, 16 * 8)
                    wait_for(act, tx_ready, 2 * q + b + 1)
                    wait_for(act, pool_ready, q - 3)
                    wait_for(act, tx_stats, 2 * (q - 3))
                    place = (x1t_even, x1t_odd)[b][(quad + 1) % 4]
                    act.activation(place.rearrange("p k c -> p (k c)"), pst, ACT.Copy).then_inc(tx_copied, 1)

                if early:
                    scaled_y(0)
                if last_:
                    wait_for(act, pt_ready, p - 1)
                    act.activation(pooled[:, bass.ds(2 * (p - 2), 2), :].rearrange("p b e -> p (b e)"),
                                   banks(2, 1)[:, 0:P], ACT.Copy).then_inc(pt_taken, 1)
                if early:
                    scaled_y(1)
                    copy_x1(p + 1, 0)
                if mid:
                    wait_for(act, nb_ready, p + 1)
                    wait_for(act, m_ready, p)
                    wait_for(act, inv_ready, p)
                    act.activation(ex, pslt, ACT.Exp, bias=small[:, 1:2], accum_out=small[:, 2:3]).then_inc(e_done, 1)
                    act.activation(ex8, mx8, ACT.Exp, bias=small[:, 1:2]).then_inc(e8_done, 1)
                if early:
                    copy_x1(p + 1, 1)
                if late:
                    wait_for(act, pool_ready, p)
                    wait_for(act, inv_ready, p)
                    wait_for(act, pt_ready, p - 1)
                    act.activation(pl_raw, psy[:, 0:P], ACT.Identity, scale=inv[:, bass.ds(p - 1, 1)],
                                   accum_out=pl_sum[:, 0:1]).then_inc(pl_step, 1)
                    wait_for(act, pl_step, 2 * p - 1)
                    act.activation(pl_sum[:, 1:2], pl_sum[:, 0:1], ACT.Identity, scale=-1.0 / P).then_inc(pl_step, 1)
                    wait_for(act, pl_step, 2 * p)
                    act.activation(pl, pl_raw, ACT.Identity, bias=pl_sum[:, 1:2]).then_inc(pl_done, 1)

            act.wait_ge(bn_step, 6)
            run_phase2(act, step)

            psh = [banks(2, 2).rearrange("p (k b) -> p k b", k=HC), banks(4, 2).rearrange("p (k b) -> p k b", k=HC)]

            def expert(e, j, i, more):
                wait_for(act, o_ready, e - 1)
                for k in range(HC):
                    wait_for(act, h_ready, HC * e + 2 * (k // 2) + 2)
                    act.activation(hb[i % 2][:, k, :], psh[i % 2][:, k, 0:B], ACT.Gelu,
                                   bias=b1t[:, k, bass.ds(e, 1)]).then_inc(g_ready, 1)

            run_phase3(act, expert)

            trp = [banks(0, 1)[:, 0:P], banks(1, 1)[:, 0:P]]

            def step4(p, j, i, first):
                par = i % 2
                wait_for(act, tr_ready, p + 1)
                wait_for(act, f_ready, 2 * (p - 1))
                act.activation(oe[par], trp[par], ACT.Copy, scale=inv[:, bass.ds(p, 1)]).then_inc(oe_done, 1)
                if first > 0:
                    store(p - 1, (i - 1) % RING)

            def store(p, i):
                wait_for(act, added, 2 * p + 2)
                act.dma_start(out_c[bass.ds(2 * p, 2), :, :].rearrange("b c s -> c b s"), x4[i]).then_inc(out_here[i], 16)

            run_phase4(act, step4)
            store(NP - 1, RING - 1)

        @block.vector
        def _(dve):
            psx = [banks(0, 2).rearrange("p (k c) -> p k c", k=NWB), banks(2, 2).rearrange("p (k c) -> p k c", k=NWB)]

            dve.memset(ones[:, :], 1.0).then_inc(ones_done, 1)
            dve.memset(neg_half[:, :], -0.5).then_inc(ones_done, 1)
            dve.wait_ge(p_here, 16)
            dve.transpose(p_cols, p_rows).then_inc(p_turned, 1)
            dve.wait_ge(ident_done, 2)
            dve.reduce_sum(col_mask[:, :], ident[:, :].rearrange("p (k q) -> p q k", q=WQ), AX.X).then_inc(p_turned, 1)
            dve.wait_ge(p_turned, 2)

            def image_stats(g, i):
                n = g * GB + i
                q = i % 2
                wait_for(dve, ln_rdone, n - 1)
                wait_for(dve, x_half, n + 1)
                for k in range(0, NWB, 2):
                    if k == NWB // 2:
                        wait_for(dve, x_turned, n + 1)
                    last = dve.bn_stats(ln_st[q][:, k:k + 2, :].rearrange("p k t -> p (k t)"),
                                        psx[q][:, k:k + 2, :].rearrange("p k c -> p c k"))
                last.then_inc(ln_stats, 1)
                wait_for(dve, ln_stats, n + 1)
                wait_for(dve, ln_ndone, n - 1)
                dve.tensor_scalar(ln_neg[q][:, :], ln_st[q][:, :, 1], -1.0, None, ALU.mult).then_inc(ln_m, 1)
                dve.tensor_scalar(ln_var[q][:, :], ln_st[q][:, :, 2], 1.0 / P, EPS_C,
                                  ALU.mult, ALU.add).then_inc(ln_v, 1)

            def stage(gc, cp, gf, fp):
                if isinstance(gf, int) and gf == 0:
                    image_stats(0, 0)
                def leaky(i):
                    wait_for(dve, v_done, gc * NCH + i + 1)
                    chunk = grp[cp][:, :, i * CH:i * CH + CH, :].rearrange("p b c w -> p b (c w)")
                    dve.scalar_tensor_tensor(out=chunk, in0=chunk, scalar=NEG_SLOPE, in1=chunk,
                                             op0=ALU.mult, op1=ALU.max).then_inc(y_done, 1)

                def stats_of_y(i):
                    if i == 0 and not (isinstance(gc, int) and gc < 2):
                        wait_for(dve, y_acc, 3 * (gc - 1))
                    wait_for(dve, y_done, gc * NCH + i + 1)
                    for c in range(i * CH, i * CH + CH, 2):
                        last = dve.bn_stats(y_st[cp][:, c:c + 2, :].rearrange("p c t -> p (c t)"),
                                            grp[cp][:, :, c:c + 2, :].rearrange("p b c w -> p b w c"))
                    last.then_inc(y_stats, 1)

                for i in range(GB):
                    if image_ahead(gf, i, 1):
                        image_stats(*image_ahead(gf, i, 1))
                    if gc is None and i % 2 == 0:
                        q = i // 2
                        dve.wait_ge(pw_spread, q + 1)
                        dve.tensor_tensor(arena_w[:, q * 2048:q * 2048 + 2048].rearrange("p (m q) -> p m q", q=WQ),
                                          banks(4 + q % 4, 1).unsqueeze(2).to_broadcast((P, 512, WQ)),
                                          col_mask[:, :].unsqueeze(1).to_broadcast((P, 512, WQ)), ALU.mult).then_inc(pw_done, 1)
                    if gc is not None and i >= 1:
                        leaky(i - 1)
                    if gc is not None and i >= 2:
                        stats_of_y(i - 2)
                if gc is not None:
                    leaky(GB - 1)
                    stats_of_y(GB - 2)
                    stats_of_y(GB - 1)

            run_phase1(dve, stage)

            dve.wait_ge(gate_here, 48)
            for i in range(4):
                wait_for(dve, y_out[i], 16 * ((G - 1) * (GB // 4)))
            dve.reduce_sum(gate_mean[0:E, 0:1], gate_rows[0:E, :], AX.X).then_inc(gate_step, 1)
            dve.wait_ge(gate_step, 1)
            dve.tensor_scalar(gate_mean[0:E, 1:2], gate_mean[0:E, 0:1], 1.0 / P, None, ALU.mult).then_inc(gate_step, 1)
            dve.wait_ge(gate_step, 2)
            dve.tensor_scalar(gate_cen[0:E, :], gate_rows[0:E, :], gate_mean[0:E, 1:2], None,
                              ALU.subtract).then_inc(gate_step, 1)

            n_part = GB * NWB
            dve.wait_ge(y_acc, 3 * G)
            dve.scalar_tensor_tensor(out=acc_sq[:, :], in0=acc_m2[:, :], scalar=1.0 / n_part, in1=acc_sq[:, :],
                                     op0=ALU.mult, op1=ALU.add).then_inc(bn_step, 1)
            dve.wait_ge(bn_sum, 1)
            dve.tensor_scalar(bn[:, 0:2], banks(0, 1)[:, 0:2], 1.0 / (P * G), None, ALU.mult).then_inc(bn_step, 1)
            dve.wait_ge(bn_step, 2)
            dve.tensor_tensor(bn[:, 2:3], bn[:, 0:1], bn[:, 0:1], ALU.mult).then_inc(bn_step, 1)
            dve.wait_ge(bn_step, 3)
            dve.tensor_tensor(bn[:, 3:4], bn[:, 1:2], bn[:, 2:3], ALU.subtract).then_inc(bn_step, 1)
            dve.wait_ge(bn_rs, 2)
            dve.tensor_tensor(bn_a, gamma_col[:, :], bn[:, 5:6], ALU.mult).then_inc(bn_step, 1)
            dve.wait_ge(bn_step, 5)
            dve.scalar_tensor_tensor(out=bn[:, 4:5], in0=bn[:, 0:1], scalar=bn_a, in1=beta_col[:, :],
                                     op0=ALU.mult, op1=ALU.subtract).then_inc(bn_rs, 1)
            dve.wait_ge(bn_rs, 3)
            dve.tensor_scalar(bn_b, bn[:, 4:5], -1.0, None, ALU.mult).then_inc(bn_step, 1)

            pst = banks(2, 2).rearrange("p (m e) -> p m e", e=E)
            psm = banks(4, 2).rearrange("p (m e) -> p m e", e=E)
            pslt = banks(6, 2)

            def wide(r):
                return r.unsqueeze(2).to_broadcast((P, 16, E))

            def step(p, ph, quad, early, mid, late, last_):
                par, o = quad % 2, 1 - quad % 2

                def stats(q, b):
                    place = x1t_even[(quad + 1) % 4] if b == 0 else x1t_odd[quad]
                    st = st2[b]
                    wait_for(dve, tx_copied, 2 * q + b + 1)
                    for k in range(0, 8, 2):
                        last = dve.bn_stats(st[:, k:k + 2, :].rearrange("p k t -> p (k t)"),
                                            place[:, k:k + 2, :].rearrange("p k c -> p c k"))
                    last.then_inc(tx_stats, 1)
                    wait_for(dve, tx_stats, 2 * q + b + 1)
                    wait_for(dve, r_ready, 2 * q + b - 1)
                    dve.tensor_scalar(var2[:, b, :], st[:, :, 2], 1.0 / P, EPS_T,
                                      ALU.mult, ALU.add).then_inc(v_ready, 1)

                if late:
                    wait_for(dve, e8_done, p)
                    wait_for(dve, m_ready, p - 1)
                    dve.memset(small[:, 4:5], 0.0)
                    dve.match_replace(out=p0, in_to_replace=ex8, in_values=ex, imm_value=0.0).then_inc(match_done, 1)
                if mid:
                    stats(p, 1)
                if late:
                    wait_for(dve, match_done, p)
                    wait_for(dve, m_out[o], 16 * (ph - (1 - par)))
                    dve.tensor_tensor(mm_[o], ex, p0, ALU.subtract).then_inc(m_ready, 1)
                if mid:
                    wait_for(dve, l_ready, p + 1)
                    wait_for(dve, r_ready, 2 * p + 2)
                    wait_for(dve, lt_ready, p)
                    dve.tensor_tensor(ls.rearrange("p k (b e) -> p (k b) e", e=E), psm, wide(r2[par]), ALU.mult).then_inc(ls_done, 1)
                if late:
                    wait_for(dve, mt_ready, p)
                    wait_for(dve, pool_ready, p - 1)
                    dve.tensor_tensor(mt.rearrange("p k (b e) -> p (k b) e", e=E), pst, wide(r2[o]), ALU.mult).then_inc(mt_taken, 1)
                if mid:
                    wait_for(dve, lt_ready, p + 1)
                    wait_for(dve, e8_done, p)
                    dve.memset(small[:, 4:5], 0.0)
                    dve.max(mx8, pslt).then_inc(max_done, 1)
                    wait_for(dve, max_done, p + 1)
                    dve.tensor_tensor(small[:, 0:1], mx8[:, 0:1], gate_b_col[:, :], ALU.add).then_inc(nb_step, 1)
                    wait_for(dve, nb_step, p + 1)
                    dve.tensor_tensor(small[:, 1:2], gate_b_col[:, :], small[:, 0:1], ALU.subtract).then_inc(nb_ready, 1)
                if early:
                    stats(p + 1, 0)
                if mid:
                    wait_for(dve, e_done, p + 1)
                    dve.reciprocal(inv[:, bass.ds(p, 1)], small[:, 2:3]).then_inc(inv_ready, 1)

            dve.wait_ge(const_here, 16 * 5)
            dve.wait_ge(bn_step, 6)
            run_phase2(dve, step)

            pso = [banks(6, 1)[:, 0:B], banks(7, 1)[:, 0:B]]

            def expert(e, j, i, more):
                wait_for(dve, o_ready, e + 1)
                dve.tensor_scalar(pooled[:, :, e], pso[i % 2], b2t[:, bass.ds(e, 1)], None, ALU.add).then_inc(o_taken, 1)

            dve.wait_ge(small_copied, 3)
            run_phase3(dve, expert)

            psf = banks(4, 4).rearrange("p (b s) -> p b s", b=2)

            def step4(p, j, i, first):
                wait_for(dve, l4_here[i], 32 * (j + 1))
                for b in range(2):
                    wait_for(dve, f_ready, 2 * p + b + 1)
                    dve.tensor_tensor(x4[i][:, b, :], psf[:, b, :], x4[i][:, b, :], ALU.add).then_inc(added, 1)

            run_phase4(dve, step4)

        @block.gpsimd
        def _(pool):
            pool.memset(ident[:, :], 0.0).then_inc(ident_done, 1)
            pool.wait_ge(ident_done, 1)
            pool.affine_select(out=ident[:, :], in_=ident[:, :], compare_op=ALU.not_equal, fill=1.0,
                               base=0, pattern=[[-1, P]], channel_multiplier=1).then_inc(ident_done, 1)
            pool.memset(spread[:, :], 0.0).then_inc(spread_done, 1)
            pool.wait_ge(spread_done, 1)
            sv = spread[:, :].rearrange("h (k q) -> h k q", q=WQ)
            pool.affine_select(out=sv, in_=sv, compare_op=ALU.not_equal, fill=1.0,
                               base=0, pattern=[[-1, S], [0, WQ]], channel_multiplier=1).then_inc(spread_done, 1)
            for a in (acc_mean, acc_m2, acc_sq):
                pool.memset(a[:, :], 0.0).then_inc(y_sq, 1)

            def image_r(g, i):
                n = g * GB + i
                q = i % 2
                wait_for(pool, ln_v, n + 1)
                wait_for(pool, norm_act, 2 * n - 2)
                pool.tensor_tensor(ln_r[q][:, :], ln_var[q][:, :], neg_half[:, 0:NWB], ALU.pow).then_inc(ln_rdone, 1)
                wait_for(pool, ln_m, n + 1)
                wait_for(pool, ln_rdone, n + 1)
                pool.tensor_tensor(ln_nmr[q][:, :], ln_neg[q][:, :], ln_r[q][:, :], ALU.mult).then_inc(ln_ndone, 1)

            def stage(gc, cp, gf, fp):
                if isinstance(gf, int) and gf == 0:
                    image_r(0, 0)
                for i in range(GB):
                    if image_ahead(gf, i, 1):
                        image_r(*image_ahead(gf, i, 1))
                if gc is not None:
                    wait_for(pool, y_stats, NCH * gc + NCH)
                    wait_for(pool, y_acc, 3 * gc)
                    mean = y_st[cp][:, :, 1]
                    pool.tensor_tensor(sq[:, :], mean, mean, ALU.mult).then_inc(y_sq, 1)
                    pool.tensor_tensor(acc_mean[:, :], acc_mean[:, :], mean, ALU.add).then_inc(y_acc, 1)
                    pool.tensor_tensor(acc_m2[:, :], acc_m2[:, :], y_st[cp][:, :, 2], ALU.add).then_inc(y_acc, 1)
                    wait_for(pool, y_sq, gc + 4)
                    pool.tensor_tensor(acc_sq[:, :], acc_sq[:, :], sq[:, :], ALU.add).then_inc(y_acc, 1)

            pool.wait_ge(ones_done, 2)
            pool.wait_ge(y_sq, 3)
            run_phase1(pool, stage)

            pool.wait_ge(bn_step, 4)
            pool.tensor_scalar(bn[:, 4:5], bn[:, 3:4], EPS_BN, None, ALU.add).then_inc(bn_rs, 1)
            pool.wait_ge(bn_rs, 1)
            pool.tensor_tensor(bn[:, 5:6], bn[:, 4:5], neg_half[:, 0:1], ALU.pow).then_inc(bn_rs, 1)

            def step(p, ph, quad, early, mid, late, last_):
                par, o = quad % 2, 1 - quad % 2
                def rstd(q, b, place):
                    wait_for(pool, mt_taken, q - 1)
                    wait_for(pool, ls_done, q - 1)
                    wait_for(pool, v_ready, 2 * q + b + 1)
                    pool.tensor_tensor(place.rearrange("p (k b) -> p b k", b=2)[:, b, :], var2[:, b, :],
                                       neg_half[:, 0:8], ALU.pow).then_inc(r_ready, 1)

                if mid:
                    rstd(p, 1, r2[par])
                if early:
                    wait_for(pool, xb_here[o], 16 * (ph + par + 1))
                    wait_for(pool, x1_out[o], 16 * (ph + par))
                    wait_for(pool, l_ready, p)
                    for b in range(2):
                        wait_for(pool, t_ready, 2 * p + 3 + b)
                        pool.tensor_tensor(x1[o][:, b, :].rearrange("p (m k) -> p m k", k=NWB),
                                           tb[b].rearrange("p (k m) -> p m k", k=NWB),
                                           xb[o][:, b, :].rearrange("p (m k) -> p m k", k=NWB),
                                           ALU.add).then_inc(x1_sum, 1)
                    rstd(p + 1, 0, r2[o])

            run_phase2(pool, step)

            pool.wait_ge(o_taken, E)

            def step4(p, j, i, first):
                par = i % 2
                wait_for(pool, tr_ready, p - 1)
                pool.tensor_copy(stg[par], pooled[:, bass.ds(2 * p, 2), :].rearrange("p b e -> p (b e)")).then_inc(stg_done, 1)

            run_phase4(pool, step4)


_INS = ['x', 'L0_conv_P', 'L0_conv_lam', 'L0_conv_gamma', 'L0_conv_beta', 'L0_ffn_gate_w', 'L0_ffn_gate_b',
        'L0_ffn_weight1', 'L0_ffn_weight2']


def kernel(**inputs):
    import numpy as _np
    import concourse.bacc as _bacc
    from concourse import mybir as _mybir
    from concourse.bass_utils import run_bass_kernel_spmd as _run

    nc = _bacc.Bacc("TRN2", target_bir_lowering=False, num_devices=1)
    arrays, args = {}, []
    for name in _INS:
        a = _np.ascontiguousarray(inputs[name])
        arrays[f"in_{name}_dram"] = a
        args.append(nc.dram_tensor(f"in_{name}_dram", a.shape, _mybir.dt.from_np(a.dtype), kind="ExternalInput").ap())
    shape = inputs['x'].shape
    args.append(nc.dram_tensor("out_0_dram", tuple(shape), _mybir.dt.float32, kind="ExternalOutput").ap())
    metaformer_kernel(nc, *args)
    r = _run(nc, [arrays], core_ids=[0])
    return r.results[0]["out_0_dram"]
```
